# Optimizing a Trainium2 kernel written in Bass

```python
import numpy as np
import jax
import jax.numpy as jnp

def _softmax(x, axis=-1):
    return jax.nn.softmax(x, axis=axis)

def _gelu(x):
    return jax.nn.gelu(x, approximate=True)

def _silu(x):
    return jax.nn.silu(x)

def _sigmoid(x):
    return jax.nn.sigmoid(x)

def _layernorm(x, axis=-1, eps=1e-05):
    m = jnp.mean(x, axis=axis, keepdims=True)
    v = jnp.var(x, axis=axis, keepdims=True)
    return (x - m) / jnp.sqrt(v + eps)

def _scatter_add(tgt, idx, src, axis=0):
    return tgt.at[idx].add(src)

def _segment_sum(src, seg, n):
    return jax.ops.segment_sum(src, seg, n)
kernel_name = 'mk_macaron_d1_jaxref_r8_6294f9'

def setup_inputs(seed: int=0):
    np.random.seed(seed)
    _w = jnp.asarray

    def _L0_attn_setup():
        import jax, jax.numpy as jnp
        import numpy as np
        N_STATE = 64
        SEQ_L = 512
        BATCH, HCH = (16, 64)
        DT_MIN, DT_MAX = (0.001, 0.1)

        def _make_DPLR_HiPPO(N):
            P = np.sqrt(1 + 2 * np.arange(N))
            A = P[:, None] * P[None, :]
            A = np.tril(A) - np.diag(np.arange(N))
            nhippo = -A
            p = 0.5 * np.sqrt(2 * np.arange(1, N + 1) + 1.0)
            q = 2 * p
            S = nhippo + p[:, None] * q[None, :]
            Lambda, V = np.linalg.eig(S)
            Vc = V.conj().T
            p_t = Vc @ p
            q_t = Vc @ q.conj()
            return (Lambda, p_t, q_t, Vc)

        def _ri(z):
            return np.stack([z.real, z.imag], axis=-1).astype(np.float32)

        def _cplx(x_ri):
            return x_ri[..., 0] + 1j * x_ri[..., 1]

        def _s4_kernel(Lambda, p, q, B, Ct, step, L):
            Omega = jnp.exp(-2j * jnp.pi * (jnp.arange(L) / L))
            g = 2.0 / step * ((1.0 - Omega) / (1.0 + Omega))
            c = 2.0 / (1.0 + Omega)
            denom = g[:, None] - Lambda[None, :]
            cauchy = lambda v: (v[None, :] / denom).sum(-1)
            k00 = cauchy(Ct.conj() * B)
            k01 = cauchy(Ct.conj() * p)
            k10 = cauchy(q.conj() * B)
            k11 = cauchy(q.conj() * p)
            at_roots = c * (k00 - k01 * (1.0 / (1.0 + k11)) * k10)
            return jnp.fft.ifft(at_roots, L).real
        key = jax.random.key(seed)
        k_u, k_ct, k_b, k_d, k_ls = jax.random.split(key, 5)
        Lambda, p, q, Vc = _make_DPLR_HiPPO(N_STATE)
        u = jax.random.normal(k_u, (BATCH, HCH, SEQ_L), dtype=jnp.float32)
        Ct_ri = jax.random.normal(k_ct, (1, N_STATE, 2), dtype=jnp.float32) / np.sqrt(N_STATE)
        Bp = jax.random.normal(k_b, (N_STATE, 1), dtype=jnp.float32) / np.sqrt(N_STATE)
        D = jax.random.uniform(k_d, (1,), dtype=jnp.float32)
        log_step = jax.random.uniform(k_ls, (1,), dtype=jnp.float32, minval=np.log(DT_MIN), maxval=np.log(DT_MAX))
        return {'u': u, 'Lambda_ri': jnp.asarray(_ri(Lambda)), 'p_ri': jnp.asarray(_ri(p)), 'q_ri': jnp.asarray(_ri(q)), 'Vc_ri': jnp.asarray(_ri(Vc)), 'Ct_ri': Ct_ri, 'Bp': Bp, 'D': D, 'log_step': log_step}
    _L0_attn_in = _L0_attn_setup()

    def _L0_ffn_setup():
        import jax, jax.numpy as jnp
        import numpy as np
        H = 512
        I = 1376
        R = 32
        NLEV = 16
        Q_ZERO = 7.5
        Q_STEP = 0.005
        LR_SCALE = 0.02

        def _qlinear(x, q, scale, A, Bm):
            w = (q.astype(jnp.float32) - Q_ZERO) * (scale * Q_STEP)[:, None]
            y = jnp.einsum('bsh,oh->bso', x, w)
            return y + LR_SCALE * (x @ A @ Bm)
        key = jax.random.key(seed)
        ks = jax.random.split(key, 13)
        B, S = (2, 256)
        inp = {'x': jax.random.normal(ks[0], (B, S, H), jnp.float32), 'gate_q': jax.random.randint(ks[1], (I, H), 0, NLEV, jnp.int32), 'gate_scale': jax.random.uniform(ks[2], (I,), jnp.float32), 'gate_A': jax.random.normal(ks[3], (H, R), jnp.float32), 'gate_B': jax.random.normal(ks[4], (R, I), jnp.float32), 'up_q': jax.random.randint(ks[5], (I, H), 0, NLEV, jnp.int32), 'up_scale': jax.random.uniform(ks[6], (I,), jnp.float32), 'up_A': jax.random.normal(ks[7], (H, R), jnp.float32), 'up_B': jax.random.normal(ks[8], (R, I), jnp.float32), 'down_q': jax.random.randint(ks[9], (H, I), 0, NLEV, jnp.int32), 'down_scale': jax.random.uniform(ks[10], (H,), jnp.float32), 'down_A': jax.random.normal(ks[11], (I, R), jnp.float32), 'down_B': jax.random.normal(ks[12], (R, H), jnp.float32)}
        return inp
    _L0_ffn_in = _L0_ffn_setup()
    _d = {'L0_attn_u': _L0_attn_in['u'], 'L0_attn_Lambda_ri': _L0_attn_in['Lambda_ri'], 'L0_attn_p_ri': _L0_attn_in['p_ri'], 'L0_attn_q_ri': _L0_attn_in['q_ri'], 'L0_attn_Vc_ri': _L0_attn_in['Vc_ri'], 'L0_attn_Ct_ri': _L0_attn_in['Ct_ri'], 'L0_attn_Bp': _L0_attn_in['Bp'], 'L0_attn_D': _L0_attn_in['D'], 'L0_attn_log_step': _L0_attn_in['log_step'], 'L0_ffn_gate_q': _L0_ffn_in['gate_q'], 'L0_ffn_gate_scale': _L0_ffn_in['gate_scale'], 'L0_ffn_gate_A': _L0_ffn_in['gate_A'], 'L0_ffn_gate_B': _L0_ffn_in['gate_B'], 'L0_ffn_up_q': _L0_ffn_in['up_q'], 'L0_ffn_up_scale': _L0_ffn_in['up_scale'], 'L0_ffn_up_A': _L0_ffn_in['up_A'], 'L0_ffn_up_B': _L0_ffn_in['up_B'], 'L0_ffn_down_q': _L0_ffn_in['down_q'], 'L0_ffn_down_scale': _L0_ffn_in['down_scale'], 'L0_ffn_down_A': _L0_ffn_in['down_A'], 'L0_ffn_down_B': _L0_ffn_in['down_B']}
    _x0 = _d['L0_attn_u']
    _d['L0_attn_u'] = jax.random.normal(jax.random.fold_in(jax.random.key(seed), 1), (2, 1024, 512), dtype=_x0.dtype)
    del _x0
    return _d

def reference(L0_attn_u, L0_attn_Lambda_ri, L0_attn_p_ri, L0_attn_q_ri, L0_attn_Vc_ri, L0_attn_Ct_ri, L0_attn_Bp, L0_attn_D, L0_attn_log_step, L0_ffn_gate_q, L0_ffn_gate_scale, L0_ffn_gate_A, L0_ffn_gate_B, L0_ffn_up_q, L0_ffn_up_scale, L0_ffn_up_A, L0_ffn_up_B, L0_ffn_down_q, L0_ffn_down_scale, L0_ffn_down_A, L0_ffn_down_B):

    def _L0_attn_ref(u, Lambda_ri, p_ri, q_ri, Vc_ri, Ct_ri, Bp, D, log_step):
        import jax, jax.numpy as jnp
        import numpy as np
        N_STATE = 64
        SEQ_L = 512
        BATCH, HCH = (16, 64)
        DT_MIN, DT_MAX = (0.001, 0.1)

        def _make_DPLR_HiPPO(N):
            P = np.sqrt(1 + 2 * np.arange(N))
            A = P[:, None] * P[None, :]
            A = np.tril(A) - np.diag(np.arange(N))
            nhippo = -A
            p = 0.5 * np.sqrt(2 * np.arange(1, N + 1) + 1.0)
            q = 2 * p
            S = nhippo + p[:, None] * q[None, :]
            Lambda, V = np.linalg.eig(S)
            Vc = V.conj().T
            p_t = Vc @ p
            q_t = Vc @ q.conj()
            return (Lambda, p_t, q_t, Vc)

        def _ri(z):
            return np.stack([z.real, z.imag], axis=-1).astype(np.float32)

        def _cplx(x_ri):
            return x_ri[..., 0] + 1j * x_ri[..., 1]

        def _s4_kernel(Lambda, p, q, B, Ct, step, L):
            Omega = jnp.exp(-2j * jnp.pi * (jnp.arange(L) / L))
            g = 2.0 / step * ((1.0 - Omega) / (1.0 + Omega))
            c = 2.0 / (1.0 + Omega)
            denom = g[:, None] - Lambda[None, :]
            cauchy = lambda v: (v[None, :] / denom).sum(-1)
            k00 = cauchy(Ct.conj() * B)
            k01 = cauchy(Ct.conj() * p)
            k10 = cauchy(q.conj() * B)
            k11 = cauchy(q.conj() * p)
            at_roots = c * (k00 - k01 * (1.0 / (1.0 + k11)) * k10)
            return jnp.fft.ifft(at_roots, L).real
        L = u.shape[-1]
        Lambda = _cplx(Lambda_ri)
        p = _cplx(p_ri)
        q = _cplx(q_ri)
        Vc = _cplx(Vc_ri)
        Ct = _cplx(Ct_ri).reshape(-1)
        B = (Vc @ Bp.astype(Vc.dtype)).reshape(-1)
        step = jnp.exp(log_step)[0]
        K = _s4_kernel(Lambda, p, q, B, Ct, step, L).astype(u.dtype)
        n = 2 * L
        y = jnp.fft.irfft(jnp.fft.rfft(u, n=n) * jnp.fft.rfft(K, n=n), n=n)[..., :L]
        return y + D[0] * u

    def _L0_ffn_ref(x, gate_q, gate_scale, gate_A, gate_B, up_q, up_scale, up_A, up_B, down_q, down_scale, down_A, down_B):
        import jax, jax.numpy as jnp
        import numpy as np
        H = 512
        I = 1376
        R = 32
        NLEV = 16
        Q_ZERO = 7.5
        Q_STEP = 0.005
        LR_SCALE = 0.02

        def _qlinear(x, q, scale, A, Bm):
            w = (q.astype(jnp.float32) - Q_ZERO) * (scale * Q_STEP)[:, None]
            y = jnp.einsum('bsh,oh->bso', x, w)
            return y + LR_SCALE * (x @ A @ Bm)
        g = _qlinear(x, gate_q, gate_scale, gate_A, gate_B)
        u = _qlinear(x, up_q, up_scale, up_A, up_B)
        h = jax.nn.silu(g) * u
        return _qlinear(h, down_q, down_scale, down_A, down_B)
    x = L0_attn_u
    x = x + 0.5 * _L0_ffn_ref(_layernorm(x, axis=-1), L0_ffn_gate_q, L0_ffn_gate_scale, L0_ffn_gate_A, L0_ffn_gate_B, L0_ffn_up_q, L0_ffn_up_scale, L0_ffn_up_A, L0_ffn_up_B, L0_ffn_down_q, L0_ffn_down_scale, L0_ffn_down_A, L0_ffn_down_B)
    x = x + _L0_attn_ref(_layernorm(x, axis=-1), L0_attn_Lambda_ri, L0_attn_p_ri, L0_attn_q_ri, L0_attn_Vc_ri, L0_attn_Ct_ri, L0_attn_Bp, L0_attn_D, L0_attn_log_step)
    x = x + 0.5 * _L0_ffn_ref(_layernorm(x, axis=-1), L0_ffn_gate_q, L0_ffn_gate_scale, L0_ffn_gate_A, L0_ffn_gate_B, L0_ffn_up_q, L0_ffn_up_scale, L0_ffn_up_A, L0_ffn_up_B, L0_ffn_down_q, L0_ffn_down_scale, L0_ffn_down_A, L0_ffn_down_B)
    return x

_drawn_inputs = setup_inputs


def setup_inputs(seed=0):
    import zlib

    import numpy as np

    out = dict(_drawn_inputs(seed))
    spreads = {}
    factors = {'L0_attn_Lambda_ri': 8.0,
     'L0_attn_p_ri': 8.0,
     'L0_attn_q_ri': 8.0,
     'L0_attn_Vc_ri': 8.0,
     'L0_attn_Ct_ri': 8.0,
     'L0_attn_Bp': 8.0}
    for name, (base, spread) in spreads.items():
        noise = np.random.default_rng([zlib.crc32(name.encode()), seed]).standard_normal(out[name].shape)
        drawn = base * np.exp(spread * noise) if base else spread * noise
        out[name] = jnp.asarray(drawn.astype(out[name].dtype))
    for name, factor in factors.items():
        out[name] = (out[name] * factor).astype(out[name].dtype)
    return out
```

```python
from contextlib import ExitStack

import concourse.bass as bass
from concourse import mybir

ALU = mybir.AluOpType
ACT = mybir.ActivationFunctionType
F32, F16, I32 = mybir.dt.float32, mybir.dt.float16, mybir.dt.int32

P = 128
Q_ZERO, Q_STEP, LR_SCALE, EPS = 7.5, 0.005, 0.02, 1e-5
Z_SCALE = 2.0 ** 11
A_SCALE = B_SCALE = 2.0 ** 8
P_SCALE = 2.0 ** 4
H_SCALE = 2.0 ** 2
S4_RESOLVENT_STEPS = 15
CHUNKS = [(0, 2), (2, 5), (5, 8), (8, 11)]


def s4_macaron(nc, x_d, lam_d, p_d, q_d, vct_d, ct_d, bp_d, dd_d, ls_d,
               gq_d, gs_d, ga_d, gb_d, uq_d, us_d, ua_d, ub_d, dq_d, ds_d, da_d, db_d,
               omega_d, opk_d, tab_d, out_d):
    T, H = x_d.shape
    I = gq_d.shape[1]
    R = ga_d.shape[1]
    NS = lam_d.shape[0]
    KH = H // P
    M = -(-I // P)
    LAST = I - (M - 1) * P
    SUBS = T // P
    TILES = T // 512
    TS = 4
    L = H
    rows = [P] * (M - 1) + [LAST]
    EVEN, ODD = (M + 1) // 2, M // 2
    x_v = x_d.rearrange("(s p) h -> p s h", p=P)
    out_v = out_d.rearrange("(s p) h -> p s h", p=P)

    def uses(n, m):
        return n * (EVEN if m % 2 == 0 else ODD) + m // 2

    with ExitStack() as ctx:
        def sb(name, shape, dt=F32):
            return ctx.enter_context(nc.sbuf_tensor(name, shape, dt))

        def sem(name):
            return ctx.enter_context(nc.semaphore(name))

        bank = [ctx.enter_context(nc.psum_tensor(f"bank{i}", [P, 512], F32)) for i in range(8)]

        X = sb("X", [P, SUBS, H])
        gq_raw = sb("gq_raw", [P, KH, I], I32)
        uq_raw = sb("uq_raw", [P, KH, I], I32)
        dq_raw = sb("dq_raw", [P, M, H], I32)
        gw = sb("gw", [P, KH, I], F16)
        uw = sb("uw", [P, KH, I], F16)
        dw = sb("dw", [P, M, H], F16)
        a_w = sb("a_w", [P, KH, 4 * R], F16)
        da_w = sb("da_w", [P, M, 2 * R], F16)
        gb_w = sb("gb_w", [P, I], F16)
        ub_w = sb("ub_w", [P, I], F16)
        db_w = sb("db_w", [P, H], F16)
        g_scale = sb("g_scale", [P, M])
        u_scale = sb("u_scale", [P, M])
        d_scale = sb("d_scale", [P, H])
        xT = sb("xT", [P, 2, KH, 512], F16)
        PT = sb("PT", [P, 2, 512], F16)
        hT = sb("hT", [P, M, 2, 512], F16)
        stats = sb("stats", [P, 2, 6])
        meanvar = sb("meanvar", [P, 2, 2])
        veps = sb("veps", [P, 2, 1])
        rstd = sb("rstd", [P, 2, 1])
        minus_half = sb("minus_half", [P, 1])
        zs = sb("zs", [P, 2, H])
        z16 = sb("z16", [P, 2, 2, H], F16)
        p_lo = sb("p_lo", [P, 2 * R])
        p32 = sb("p32", [P, 2 * R])
        p_stack = sb("p_stack", [P, 2, 4, R], F16)
        pd_lo = sb("pd_lo", [P, R])
        pd32 = sb("pd32", [P, R])
        pd_stack = sb("pd_stack", [P, 4, R], F16)
        PdT = sb("PdT", [P, P], F16)
        ident = sb("ident", [P, P])
        ident16 = sb("ident16", [P, P], F16)
        lam = sb("lam", [NS, 2])
        nlam = sb("nlam", [NS, 2])
        pv = sb("pv", [NS, 2])
        lv = sb("lv", [NS, 2, 2])
        bp = sb("bp", [NS, 1])
        log_step = sb("log_step", [NS, 1])
        a_step = sb("a_step", [NS, 2])
        rr = sb("rr", [NS, 2, 2])
        w1 = sb("w1", [NS, 8])
        w2 = sb("w2", [NS, 8])
        vt = sb("vt", [NS, 2, 2])
        cs = sb("cs", [P, KH, 8])
        opk = sb("opk", [P, 2, KH])
        cw = sb("cw", [P, 16, KH])
        d_col = sb("d_col", [P, 2])
        work = sb("work", [P, 12, 512])

        def parts(tensor, shapes):
            names = "pabc"[:len(tensor.shape)]
            flat = tensor[tuple(slice(0, d) for d in tensor.shape)]
            if len(tensor.shape) > 2:
                flat = flat.rearrange(f"{' '.join(names)} -> p ({' '.join(names[1:])})")
            flat = flat.bitcast(F32)
            pos, out = 0, []
            for n, *free in shapes:
                half = free[0] == "16"
                free = free[1:] if half else free
                size = 1
                for d in free:
                    size *= d
                words = size // 2 if half else size
                piece = flat[0:n, pos:pos + words]
                pos += words
                if half:
                    piece = piece.bitcast(F16)
                if len(free) > 1:
                    dims = "abc"[:len(free)]
                    piece = piece.rearrange(f"p ({' '.join(dims)}) -> p {' '.join(dims)}",
                                            **dict(zip(dims[1:], free[1:])))
                out.append(piece)
            return out

        tg, tu, g32, u32, silu, h32 = parts(work, [(P, 2, 512)] * 6)
        b_raw, db_raw, da_raw, b_hi, a_raw, vct = parts(
            work, [(P, 2, I), (P, H), (P, M, R), (P, "16", I), (P, KH, 2 * R), (NS, 2, NS)])
        omega, den, dsq, res = parts(hT, [(NS, 3, L), (NS, 2, L), (NS, 2, L), (NS, 2, L)])
        tab, = parts(gq_raw, [(P, 2, KH, L)])
        phase, ptmp, toep, zT, dtmp, dsum = parts(
            uq_raw, [(P, 2, KH, P), (P, 2, P), (P, L), (P, 2, KH, P), (P, 2, H), (P, H)])

        s_x = [sem(f"x_sub{j}_loaded") for j in range(TS)]
        s_xrest = sem("x_rest_loaded")
        s_q = [sem(f"gate_up_chunk{c}_loaded") for c in range(len(CHUNKS))]
        s_dq = sem("down_loaded")
        s_small = sem("small_loaded")
        s_lr = sem("low_rank_a_loaded")
        s_lrb = sem("low_rank_rest_loaded")
        s_kin = sem("s4_inputs_loaded")
        s_tab = sem("tables_loaded")
        s_out = sem("out_stored")
        s_const = sem("constants_ready")
        s_ident = sem("identities_ready")
        s_gucast = sem("gate_up_cast")
        s_dcast = sem("down_cast")
        s_scales = sem("scales_ready")
        s_hi = sem("weight_hi_parts_ready")
        s_aw = sem("low_rank_a_ready")
        s_lrw = sem("low_rank_rest_ready")
        s_k = sem("dve_s4_step")
        s_bmm = sem("s4_b_mm")
        s_exp = sem("s4_step_exp")
        s_cauchy = sem("s4_cauchy_mm")
        s_phase = sem("s4_phase_ready")
        s_toep = sem("s4_toeplitz_mm")
        s_tcopy = sem("s4_toeplitz_copied")
        s_masked = sem("s4_toeplitz_masked")

        class Stage:

            def __init__(self, name):
                def s(what):
                    return sem(f"{name}_{what}")

                def two(what):
                    return [s(f"{what}_{b}") for b in range(2)]

                self.agg, self.var = two("agg"), two("var")
                self.rstd, self.zs, self.zhi, self.z16 = two("rstd"), two("zs"), two("zhi"), two("z16")
                self.z_used = self.z16
                self.tp, self.xT = s("x_transposed"), s("xT_ready")
                self.p_mm, self.p_lo, self.p32 = s("p_mm"), s("p_lo"), s("p32")
                self.p_hi, self.p_stack = s("p_hi"), s("p_stack")
                self.p_t, self.p_out = s("p_transposed"), s("p_transposed_out")
                self.pd_t, self.pd_out = s("pd_transposed"), s("pd_transposed_out")
                self.g_mm, self.gl_mm, self.u_mm, self.ul_mm = s("g_mm"), s("gl_mm"), s("u_mm"), s("ul_mm")
                self.tg, self.tu, self.g, self.u = two("tg"), two("tu"), two("g"), two("u")
                self.silu, self.h, self.hhi, self.hlo = two("silu"), two("h"), two("hhi"), two("hlo")
                self.d_mm, self.d_read = two("d_mm"), two("d_read")
                self.pd_lo, self.pd32, self.pd_hi, self.pd_stack = s("pd_lo"), s("pd32"), s("pd_hi"), s("pd_stack")
                self.dl_mm, self.dsum, self.x_out = s("dl_mm"), s("dsum"), s("x_updated")

        f_sems = Stage("ffn")

        c_agg = [sem(f"conv_agg_{b}") for b in range(2)]
        c_var = [sem(f"conv_var_{b}") for b in range(2)]
        c_rstd = [sem(f"conv_rstd_{b}") for b in range(2)]
        c_zs = [sem(f"conv_zs_{b}") for b in range(2)]
        c_tp = [sem(f"conv_transposed_{b}") for b in range(2)]
        c_zT = [sem(f"conv_zT_{b}") for b in range(2)]
        c_mm = [sem(f"conv_mm_{b}") for b in range(2)]
        c_out = [sem(f"conv_out_{b}") for b in range(2)]

        block = ctx.enter_context(nc.Block())

        def at(s):
            return X[:, bass.ds(s, 1), :].rearrange("p a h -> p (a h)")

        @block.sync
        def _(sp):
            for j in range(TS):
                sp.dma_start(X[:, j, :], x_v[:, j, :]).then_inc(s_x[j], 16)
            gq_v = gq_d.rearrange("(k p) i -> p k i", p=P)
            uq_v = uq_d.rearrange("(k p) i -> p k i", p=P)
            for c, (m0, m1) in enumerate(CHUNKS):
                cols = slice(m0 * P, min(m1 * P, I))
                sp.dma_start(gq_raw[:, :, cols], gq_v[:, :, cols]).then_inc(s_q[c], 16)
                sp.dma_start(uq_raw[:, :, cols], uq_v[:, :, cols]).then_inc(s_q[c], 16)
            sp.dma_start(dq_raw[:, 0:M - 1, :],
                         dq_d[0:(M - 1) * P, :].rearrange("(m p) h -> p m h", p=P)).then_inc(s_dq, 16)
            sp.dma_start(dq_raw[0:LAST, M - 1, :], dq_d[(M - 1) * P:I, :]).then_inc(s_dq, 16)
            sp.dma_start(X[:, TS:SUBS, :], x_v[:, TS:SUBS, :]).then_inc(s_xrest, 16)
            sp.wait_ge(s_gucast, len(CHUNKS))
            sp.dma_start(tab, tab_d.rearrange("c (k p) m -> p c k m", p=P)).then_inc(s_tab, 16)

            with sp.Fori(0, SUBS) as s:
                sp.wait_ge(f_sems.x_out, s + (SUBS + 1))
                sp.dma_start(out_v[:, bass.ds(s, 1), :], X[:, bass.ds(s, 1), :]).then_inc(s_out, 16)
            sp.wait_ge(s_out, 16 * SUBS)

        @block.gpsimd
        def _(pool):
            pool.memset(minus_half[:, :], -0.5).then_inc(s_const, 1)
            pool.memset(ident[:, :], 0.0).then_inc(s_const, 1)
            pool.memset(ident16[:, :], 0.0).then_inc(s_const, 1)
            pool.wait_ge(s_const, 3)
            for m in (ident, ident16):
                pool.affine_select(out=m[:, :], in_=m[:, :], compare_op=ALU.not_equal, fill=1.0, base=0,
                                   pattern=[[-1, P]], channel_multiplier=1).then_inc(s_ident, 1)

            def ln_rstd(f, b, k):
                pool.wait_ge(f.var[b], k + 1)
                pool.tensor_tensor(rstd[:, b, :], veps[:, b, :], minus_half[:, :], ALU.pow)\
                    .then_inc(f.rstd[b], 1)

            def cast_weights():
                for c, (m0, m1) in enumerate(CHUNKS):
                    cols = slice(m0 * P, min(m1 * P, I))
                    pool.wait_ge(s_q[c], 32)
                    pool.tensor_scalar(gw[:, :, cols], gq_raw[:, :, cols], -Q_ZERO, 1.0, ALU.add, ALU.mult)
                    pool.tensor_scalar(uw[:, :, cols], uq_raw[:, :, cols], -Q_ZERO, 1.0, ALU.add, ALU.mult)\
                        .then_inc(s_gucast, 1)
                pool.wait_ge(s_dq, 32)
                for m in range(M):
                    pool.tensor_scalar(dw[0:rows[m], m, :], dq_raw[0:rows[m], m, :], -Q_ZERO, 1.0,
                                       ALU.add, ALU.mult).then_inc(s_dcast, 1)

            def ffn_stage(f, base):
                for j in range(TS):
                    ln_rstd(f, j % 2, base * 2 + j // 2)
                if base == 0:
                    cast_weights()
                with pool.Fori(base + 1, base + TILES) as n:
                    for j in range(TS):
                        ln_rstd(f, j % 2, n * 2 + j // 2)

            ffn_stage(f_sems, 0)
            pool.wait_ge(s_tcopy, 1)
            pool.affine_select(out=toep[:, 0:P], in_=toep[:, 0:P], compare_op=ALU.is_ge, fill=0.0, base=0,
                               pattern=[[1, P]], channel_multiplier=-1).then_inc(s_masked, 1)
            with pool.Fori(1, SUBS // 2 + 1) as i:
                for b in range(2):
                    pool.wait_ge(c_var[b], i)
                    pool.tensor_tensor(rstd[:, b, :], veps[:, b, :], minus_half[:, :], ALU.pow)\
                        .then_inc(c_rstd[b], 1)
            ffn_stage(f_sems, TILES)

        @block.scalar
        def _(act):
            act.dma_start(a_raw[:, :, 0:R], ga_d.rearrange("(k p) r -> p k r", p=P)).then_inc(s_lr, 16)
            act.dma_start(a_raw[:, :, R:2 * R], ua_d.rearrange("(k p) r -> p k r", p=P)).then_inc(s_lr, 16)
            act.dma_start(lam[:, :], lam_d).then_inc(s_kin, 16)
            act.dma_start(pv[:, :], p_d).then_inc(s_kin, 16)
            act.dma_start(lv[:, 0, :], ct_d).then_inc(s_kin, 16)
            act.dma_start(lv[:, 1, :], q_d).then_inc(s_kin, 16)
            act.dma_start(vct[:, :, :], vct_d.rearrange("c m n -> m c n")).then_inc(s_kin, 16)
            act.dma_start(bp[:, :], bp_d).then_inc(s_kin, 16)
            act.dma_start(log_step[:, :], ls_d.partition_broadcast(NS)).then_inc(s_kin, 16)
            act.dma_start(omega[:, :, :], omega_d.partition_broadcast(NS)).then_inc(s_kin, 16)
            act.dma_start(opk[:, :, :], opk_d).then_inc(s_kin, 16)
            act.dma_start(d_col[:, 0:1], dd_d.partition_broadcast(P)).then_inc(s_kin, 16)
            act.dma_start(g_scale[:, :], gs_d).then_inc(s_small, 16)
            act.dma_start(u_scale[:, :], us_d).then_inc(s_small, 16)
            act.dma_start(d_scale[:, :], ds_d.partition_broadcast(P)).then_inc(s_small, 16)
            for g in range(4):
                act.dma_start(b_raw[g * R:(g + 1) * R, 0, :], gb_d).then_inc(s_lrb, 16)
                act.dma_start(b_raw[g * R:(g + 1) * R, 1, :], ub_d).then_inc(s_lrb, 16)
                act.dma_start(db_raw[g * R:(g + 1) * R, :], db_d).then_inc(s_lrb, 16)
            act.dma_start(da_raw[:, 0:M - 1, :],
                          da_d[0:(M - 1) * P, :].rearrange("(m p) r -> p m r", p=P)).then_inc(s_lrb, 16)
            act.dma_start(da_raw[0:LAST, M - 1, :], da_d[(M - 1) * P:I, :]).then_inc(s_lrb, 16)
            act.wait_ge(s_kin, 160)
            nc.scalar.activation(a_step[:, 0:1], log_step[:, :], ACT.Exp, scale=-1.0).then_inc(s_exp, 1)

            def p_low(f, k):
                act.wait_ge(f.p_mm, k + 1)
                act.wait_ge(f.p32, k)
                nc.scalar.activation(p_lo[:, :], bank[2][:, 2 * R:4 * R], ACT.Copy,
                                     scale=P_SCALE / (Z_SCALE * A_SCALE)).then_inc(f.p_lo, 1)

            def p_out(f, j, k):
                act.wait_ge(f.p_t, k + 1)
                nc.scalar.activation(PT[:, :, j * P:(j + 1) * P],
                                     bank[7][:, 0:P].bitcast(F16).rearrange("p (a t) -> p a t", a=2),
                                     ACT.Copy).then_inc(f.p_out, 1)

            def ffn_stage(f, base):
                def scaled(out, in_, scale, m):
                    return nc.scalar.activation(out, in_, ACT.Copy, scale=scale[0:rows[m], m:m + 1])

                def h_high(n, m):
                    b, r = m % 2, rows[m]
                    act.wait_ge(f.h[b], uses(n, m) + 1)
                    nc.scalar.activation(hT[0:r, m, 0, :], h32[0:r, b, :], ACT.Copy, scale=H_SCALE)\
                        .then_inc(f.hhi[b], 1)

                def hidden(n):
                    for m in range(M):
                        b, r, k = m % 2, rows[m], uses(n, m)
                        act.wait_ge(f.g_mm, n * M + m + 1)
                        act.wait_ge(f.g[b], k)
                        scaled(tg[0:r, b, :], bank[0][0:r, :], g_scale, m).then_inc(f.tg[b], 1)
                        if m:
                            h_high(n, m - 1)
                        act.wait_ge(f.g[b], k + 1)
                        act.wait_ge(f.h[b], k)
                        nc.scalar.activation(silu[0:r, b, :], g32[0:r, b, :], ACT.Silu).then_inc(f.silu[b], 1)
                        act.wait_ge(f.u_mm, n * M + m + 1)
                        act.wait_ge(f.u[b], k)
                        scaled(tu[0:r, b, :], bank[1][0:r, :], u_scale, m).then_inc(f.tu[b], 1)
                    h_high(n, M - 1)

                def pd_low(n, j):
                    b = j % 2
                    act.wait_ge(f.d_mm[b], n * 2 + j // 2 + 1)
                    act.wait_ge(f.pd32, n * TS + j)
                    nc.scalar.activation(pd_lo[:, :], bank[b][:, R:2 * R], ACT.Copy,
                                         scale=1.0 / (H_SCALE * A_SCALE)).then_inc(f.pd_lo, 1)

                def pd_out(n, j):
                    act.wait_ge(f.pd_t, n * TS + j + 1)
                    act.wait_ge(f.dl_mm, n * TS + j)
                    nc.scalar.activation(PdT[:, :], bank[7][:, 0:P // 2].bitcast(F16), ACT.Copy)\
                        .then_inc(f.pd_out, 1)

                def tile(n, more):
                    hidden(n)
                    for j in range(TS + 2):
                        if j < TS:
                            pd_low(n, j)
                        if 1 <= j <= TS:
                            pd_out(n, j - 1)
                            if more:
                                p_low(f, (n + 1) * TS + j - 1)
                        if more and j >= 2:
                            p_out(f, j - 2, (n + 1) * TS + j - 2)

                k0 = base * TS
                for j in range(TS + 2):
                    if 1 <= j <= TS:
                        p_low(f, k0 + j - 1)
                    if j >= 2:
                        p_out(f, j - 2, k0 + j - 2)
                if base == 0:
                    act.wait_ge(s_scales, 3)
                if base == 0:
                    tile(0, True)
                with act.Fori(max(base, 1), base + TILES - 1) as n:
                    tile(n, True)
                if base == 0:
                    act.wait_ge(s_toep, 1)
                    nc.scalar.activation(toep[:, :], bank[6][:, :], ACT.Copy).then_inc(s_tcopy, 1)
                tile(base + TILES - 1, False)

            ffn_stage(f_sems, 0)

            def conv_evacuate(i):
                for b in range(2):
                    act.wait_ge(c_tp[b], i + 1)
                    act.wait_ge(c_mm[b], i)
                    nc.scalar.activation(zT[:, b, :, :], bank[b][:, :].rearrange("p (k t) -> p k t", k=KH),
                                         ACT.Copy).then_inc(c_zT[b], 1)

            conv_evacuate(0)
            with act.Fori(1, SUBS // 2) as i:
                conv_evacuate(i)
            ffn_stage(f_sems, TILES)

        @block.vector
        def _(dve):
            V = nc.vector

            def ln_stats(f, b, k, s):
                dve.wait_ge(f.agg[b], k)
                dve.wait_ge(f.zs[b], k)
                V.bn_stats(stats[:, b, :], at(s))
                dve.drain()
                V.bn_aggr(meanvar[:, b, :], stats[:, b, :]).then_inc(f.agg[b], 1)
                dve.wait_ge(f.agg[b], k + 1)
                V.tensor_scalar(veps[:, b, :], meanvar[:, b, 1:2], EPS, 1.0 / Z_SCALE ** 2,
                                ALU.add, ALU.mult).then_inc(f.var[b], 1)

            def ln_apply(f, b, k, s):
                dve.wait_ge(f.z_used[b], k)
                dve.wait_ge(f.rstd[b], k + 1)
                V.tensor_scalar(zs[:, b, :], at(s), meanvar[:, b, 0:1], rstd[:, b, :],
                                ALU.subtract, ALU.mult).then_inc(f.zs[b], 1)

            def z_parts(f, b, k):
                dve.wait_ge(f.zs[b], k + 1)
                V.tensor_copy(z16[:, b, 0, :], zs[:, b, :]).then_inc(f.zhi[b], 1)
                dve.wait_ge(f.zhi[b], k + 1)
                V.tensor_tensor(z16[:, b, 1, :], zs[:, b, :], z16[:, b, 0, :], ALU.subtract)\
                    .then_inc(f.z16[b], 1)

            def x_out(f, j, k):
                dve.wait_ge(f.tp, k + 1)
                V.tensor_copy(xT[:, :, :, j * P:(j + 1) * P],
                              bank[3][:, :].bitcast(F16).rearrange("p (a k t) -> p a k t", a=2, k=KH))\
                    .then_inc(f.xT, 1)

            def p_split(f, k):
                dve.wait_ge(f.p_lo, k + 1)
                dve.wait_ge(f.p_stack, k)
                V.scalar_tensor_tensor(p32[:, :], bank[2][:, 0:2 * R], P_SCALE / (Z_SCALE * A_SCALE),
                                       p_lo[:, :], ALU.mult, ALU.add).then_inc(f.p32, 1)
                dve.wait_ge(f.p32, k + 1)
                dve.wait_ge(f.p_t, k)
                p2 = p32[:, :].rearrange("p (g r) -> p g r", g=2)
                V.tensor_copy(p_stack[:, :, 0, :], p2)
                V.tensor_copy(p_stack[:, :, 2, :], p2).then_inc(f.p_hi, 1)
                dve.wait_ge(f.p_hi, k + 1)
                V.tensor_tensor(p_stack[:, :, 1, :], p2, p_stack[:, :, 0, :], ALU.subtract)
                V.tensor_tensor(p_stack[:, :, 3, :], p2, p_stack[:, :, 0, :], ALU.subtract)\
                    .then_inc(f.p_stack, 1)

            def ffn_stage(f, base):
                def h_low(n, m):
                    b, r = m % 2, rows[m]
                    dve.wait_ge(f.hhi[b], uses(n, m) + 1)
                    V.scalar_tensor_tensor(hT[0:r, m, 1, :], h32[0:r, b, :], H_SCALE, hT[0:r, m, 0, :],
                                           ALU.mult, ALU.subtract).then_inc(f.hlo[b], 1)

                def hidden(n):
                    c = LR_SCALE / (P_SCALE * B_SCALE)
                    for m in range(M):
                        b, r, k = m % 2, rows[m], uses(n, m)
                        dve.wait_ge(f.tg[b], k + 1)
                        dve.wait_ge(f.gl_mm, n * M + m + 1)
                        dve.wait_ge(f.silu[b], k)
                        V.scalar_tensor_tensor(g32[0:r, b, :], bank[2][0:r, :], c, tg[0:r, b, :],
                                               ALU.mult, ALU.add).then_inc(f.g[b], 1)
                        if m:
                            h_low(n, m - 1)
                        dve.wait_ge(f.tu[b], k + 1)
                        dve.wait_ge(f.ul_mm, n * M + m + 1)
                        dve.wait_ge(f.h[b], k)
                        V.scalar_tensor_tensor(u32[0:r, b, :], bank[3][0:r, :], c, tu[0:r, b, :],
                                               ALU.mult, ALU.add).then_inc(f.u[b], 1)
                        dve.wait_ge(f.u[b], k + 1)
                        dve.wait_ge(f.silu[b], k + 1)
                        dve.wait_ge(f.hlo[b], k)
                        V.tensor_tensor(h32[0:r, b, :], silu[0:r, b, :], u32[0:r, b, :], ALU.mult)\
                            .then_inc(f.h[b], 1)
                    h_low(n, M - 1)

                def down_read(n, j):
                    b, k = j % 2, n * TS + j
                    dve.wait_ge(f.pd_lo, k + 1)
                    dve.wait_ge(f.pd_stack, k)
                    V.scalar_tensor_tensor(pd32[:, :], bank[b][:, 0:R], 1.0 / (H_SCALE * A_SCALE),
                                           pd_lo[:, :], ALU.mult, ALU.add).then_inc(f.pd32, 1)
                    dve.wait_ge(f.pd32, k + 1)
                    dve.wait_ge(f.pd_t, k)
                    V.tensor_copy(pd_stack[:, 0, :], pd32[:, :])
                    V.tensor_copy(pd_stack[:, 2, :], pd32[:, :]).then_inc(f.pd_hi, 1)
                    dve.wait_ge(f.pd_hi, k + 1)
                    V.tensor_tensor(pd_stack[:, 1, :], pd32[:, :], pd_stack[:, 0, :], ALU.subtract)
                    V.tensor_tensor(pd_stack[:, 3, :], pd32[:, :], pd_stack[:, 0, :], ALU.subtract)\
                        .then_inc(f.pd_stack, 1)
                    V.tensor_tensor(dtmp[:, b, :], bank[4 + b][:, :], d_scale[:, :], ALU.mult)\
                        .then_inc(f.d_read[b], 1)

                def down_add(n, j):
                    b, k = j % 2, n * TS + j
                    dve.wait_ge(f.dl_mm, k + 1)
                    dve.wait_ge(f.x_out, k)
                    dve.wait_ge(f.d_read[b], n * 2 + j // 2 + 1)
                    V.scalar_tensor_tensor(dsum[:, :], bank[6][:, :], 0.5 * LR_SCALE / B_SCALE,
                                           dtmp[:, b, :], ALU.mult, ALU.add).then_inc(f.dsum, 1)
                    dve.wait_ge(f.dsum, k + 1)
                    V.tensor_tensor(at(k - base * TS), at(k - base * TS), dsum[:, :], ALU.add)\
                        .then_inc(f.x_out, 1)

                def tile(n, more):
                    hidden(n)
                    k0 = (n + 1) * TS
                    if more:
                        ln_stats(f, 0, (n + 1) * 2, k0 - base * TS)
                    for j in range(TS + 1):
                        b = j % 2
                        if more and j < TS:
                            if j + 1 < TS:
                                ln_stats(f, (j + 1) % 2, (n + 1) * 2 + (j + 1) // 2,
                                         k0 + j + 1 - base * TS)
                            ln_apply(f, b, (n + 1) * 2 + j // 2, k0 + j - base * TS)
                            dve.wait_ge(f.tp, k0 + j - 1)
                            z_parts(f, b, (n + 1) * 2 + j // 2)
                        if j < TS:
                            down_read(n, j)
                            if more:
                                x_out(f, j, k0 + j)
                        if j >= 1:
                            if more:
                                p_split(f, k0 + j - 1)
                            down_add(n, j - 1)

                k0 = base * TS
                for j in range(TS):
                    b, kb = j % 2, base * 2 + j // 2
                    if base == 0:
                        dve.wait_ge(s_x[j], 16)
                    ln_stats(f, b, kb, j)
                    ln_apply(f, b, kb, j)
                    if k0 + j >= 2:
                        dve.wait_ge(f.tp, k0 + j - 1)
                    z_parts(f, b, kb)
                    x_out(f, j, k0 + j)
                    if j >= 1:
                        p_split(f, k0 + j - 1)
                p_split(f, k0 + TS - 1)
                if base == 0:
                    s4_roots()
                    low_rank_rest()
                    dve.wait_ge(s_xrest, 16)
                if base == 0:
                    tile(0, True)
                with dve.Fori(max(base, 1), base + TILES - 1) as n:
                    tile(n, True)
                if base == 0:
                    s4_phase()
                tile(base + TILES - 1, False)

            def low_rank_a():
                dve.wait_ge(s_lr, 32)
                V.tensor_scalar(a_w[:, :, 0:2 * R], a_raw[:, :, :], A_SCALE, None, ALU.mult).then_inc(s_hi, 1)
                dve.wait_ge(s_hi, 1)
                V.scalar_tensor_tensor(a_w[:, :, 2 * R:4 * R], a_raw[:, :, :], A_SCALE, a_w[:, :, 0:2 * R],
                                       ALU.mult, ALU.subtract).then_inc(s_aw, 1)
                dve.wait_ge(s_small, 48)
                for t, c in ((g_scale, Q_STEP / Z_SCALE), (u_scale, Q_STEP / Z_SCALE),
                             (d_scale, 0.5 * Q_STEP / H_SCALE)):
                    V.tensor_scalar(t[:, :], t[:, :], c, None, ALU.mult).then_inc(s_scales, 1)
                dve.wait_ge(s_scales, 3)

            def low_rank_rest():
                dve.wait_ge(s_lrb, 224)
                stacks = ((gb_w, b_raw[:, 0, :], I), (ub_w, b_raw[:, 1, :], I), (db_w, db_raw[:, :], H))
                for n, (w, raw, cols) in enumerate(stacks):
                    V.tensor_scalar(w[0:2 * R, :], raw[0:2 * R, :], B_SCALE, None, ALU.mult)
                    dve.wait_ge(s_lrw, n)
                    V.tensor_scalar(b_hi[2 * R:4 * R, 0:cols], raw[2 * R:4 * R, :], B_SCALE, None, ALU.mult)\
                        .then_inc(s_hi, 1)
                    dve.wait_ge(s_hi, 2 + n)
                    V.scalar_tensor_tensor(w[2 * R:4 * R, :], raw[2 * R:4 * R, :], B_SCALE,
                                           b_hi[2 * R:4 * R, 0:cols], ALU.mult, ALU.subtract).then_inc(s_lrw, 1)
                for part in ((slice(0, P), slice(0, M - 1)), (slice(0, LAST), slice(M - 1, M))):
                    V.tensor_scalar(da_w[part[0], part[1], 0:R], da_raw[part[0], part[1], :], A_SCALE, None,
                                    ALU.mult).then_inc(s_hi, 1)
                dve.wait_ge(s_hi, 6)
                for part in ((slice(0, P), slice(0, M - 1)), (slice(0, LAST), slice(M - 1, M))):
                    V.scalar_tensor_tensor(da_w[part[0], part[1], R:2 * R], da_raw[part[0], part[1], :],
                                           A_SCALE, da_w[part[0], part[1], 0:R], ALU.mult, ALU.subtract)\
                        .then_inc(s_lrw, 1)

            steps = [0]

            def link(ins):
                steps[0] += 1
                ins.then_inc(s_k, 1)
                dve.wait_ge(s_k, steps[0])

            def s4_roots():
                dve.wait_ge(s_kin, 160)
                dve.wait_ge(s_bmm, 1)
                V.tensor_copy(rr[:, :, 0], bank[4][0:NS, 0:2])
                V.tensor_copy(rr[:, :, 1], pv[:, :])
                link(V.tensor_scalar(nlam[:, :], lam[:, :], -1.0, None, ALU.mult))
                for i in range(2):
                    lr, li = lv[:, i, 0:1], lv[:, i, 1:2]
                    V.tensor_scalar(vt[:, 0, :], rr[:, 1, :], li, None, ALU.mult)
                    link(V.tensor_scalar(vt[:, 1, :], rr[:, 0, :], li, None, ALU.mult))
                    V.scalar_tensor_tensor(w1[:, 2 * i:2 * i + 2], rr[:, 0, :], lr, vt[:, 0, :],
                                           ALU.mult, ALU.add)
                    link(V.scalar_tensor_tensor(w1[:, 4 + 2 * i:6 + 2 * i], rr[:, 1, :], lr, vt[:, 1, :],
                                                ALU.mult, ALU.subtract))
                V.tensor_scalar(w2[:, 0:4], w1[:, 4:8], -1.0, None, ALU.mult)
                V.tensor_copy(w2[:, 4:8], w1[:, 0:4])
                dve.wait_ge(s_exp, 1)
                link(V.tensor_scalar(a_step[:, 1:2], a_step[:, 0:1], 2.0, None, ALU.mult))
                link(V.tensor_scalar(den[:, 0, :], omega[:, 0, :], a_step[:, 1:2], None, ALU.mult))
                link(V.scalar_tensor_tensor(dsq[:, 0, :], omega[:, 1, :], nlam[:, 0:1], den[:, 0, :],
                                            ALU.mult, ALU.add))
                V.scalar_tensor_tensor(den[:, 0, :], omega[:, 2, :], lam[:, 1:2], dsq[:, 0, :],
                                       ALU.mult, ALU.add)
                link(V.tensor_tensor(a_step[:, 0:1], nlam[:, 0:1], a_step[:, 1:2], ALU.subtract))
                link(V.tensor_scalar(dsq[:, 1, :], omega[:, 2, :], a_step[:, 0:1], None, ALU.mult))
                link(V.scalar_tensor_tensor(den[:, 1, :], omega[:, 1, :], nlam[:, 1:2], dsq[:, 1, :],
                                            ALU.mult, ALU.add))
                V.tensor_tensor(dsq[:, 0, :], den[:, 0, :], den[:, 0, :], ALU.mult)
                link(V.tensor_tensor(dsq[:, 1, :], den[:, 1, :], den[:, 1, :], ALU.mult))
                link(V.tensor_tensor(dsq[:, 0, :], dsq[:, 0, :], dsq[:, 1, :], ALU.add))
                link(V.reciprocal(dsq[:, 1, :], dsq[:, 0, :]))
                V.tensor_tensor(res[:, 0, :], den[:, 0, :], dsq[:, 1, :], ALU.mult)
                link(V.scalar_tensor_tensor(res[:, 1, :], den[:, 1, :], -1.0, dsq[:, 1, :],
                                            ALU.mult, ALU.mult))
                dve.wait_ge(s_cauchy, 1)
                link(V.tensor_copy(cs[:, :, :], bank[5][:, 0:8 * KH].rearrange("p (k c) -> p k c", c=8)))

                def product(o, ar, ai, br, bi):
                    V.tensor_tensor(cw[:, 12, :], ar, br, ALU.mult)
                    V.tensor_tensor(cw[:, 13, :], ai, bi, ALU.mult)
                    V.tensor_tensor(cw[:, 14, :], ar, bi, ALU.mult)
                    link(V.tensor_tensor(cw[:, 15, :], ai, br, ALU.mult))
                    V.tensor_tensor(cw[:, o, :], cw[:, 12, :], cw[:, 13, :], ALU.subtract)
                    link(V.tensor_tensor(cw[:, o + 1, :], cw[:, 14, :], cw[:, 15, :], ALU.add))

                product(0, cs[:, :, 1], cs[:, :, 5], cs[:, :, 2], cs[:, :, 6])
                product(2, opk[:, 0, :], opk[:, 1, :], cw[:, 0, :], cw[:, 1, :])
                product(4, opk[:, 0, :], opk[:, 1, :], cs[:, :, 3], cs[:, :, 7])
                link(V.tensor_scalar(cw[:, 4, :], cw[:, 4, :], 1.0, None, ALU.add))
                V.tensor_tensor(cw[:, 6, :], cw[:, 4, :], cw[:, 4, :], ALU.mult)
                link(V.tensor_tensor(cw[:, 7, :], cw[:, 5, :], cw[:, 5, :], ALU.mult))
                link(V.tensor_tensor(cw[:, 6, :], cw[:, 6, :], cw[:, 7, :], ALU.add))
                link(V.reciprocal(cw[:, 7, :], cw[:, 6, :]))
                V.tensor_tensor(cw[:, 8, :], cw[:, 4, :], cw[:, 7, :], ALU.mult)
                link(V.scalar_tensor_tensor(cw[:, 9, :], cw[:, 5, :], -1.0, cw[:, 7, :],
                                            ALU.mult, ALU.mult))
                product(10, cw[:, 2, :], cw[:, 3, :], cw[:, 8, :], cw[:, 9, :])
                V.tensor_tensor(cw[:, 0, :], cs[:, :, 0], cw[:, 10, :], ALU.subtract)
                link(V.tensor_tensor(cw[:, 1, :], cs[:, :, 4], cw[:, 11, :], ALU.subtract))
                link(V.tensor_scalar(cw[:, 2:4, :], cw[:, 0:2, :], 2.0 / (L * Z_SCALE), None, ALU.mult))

            def s4_phase():
                dve.wait_ge(s_tab, 16)
                for k in range(KH):
                    at_r, at_i = cw[:, 2, k:k + 1], cw[:, 3, k:k + 1]
                    cos, sin = tab[:, 0, k, 0:P], tab[:, 1, k, 0:P]
                    V.tensor_scalar(ptmp[:, 0, :], sin, at_i, None, ALU.mult)
                    link(V.tensor_scalar(ptmp[:, 1, :], cos, at_i, None, ALU.mult))
                    V.scalar_tensor_tensor(phase[:, 0, k, :], cos, at_r, ptmp[:, 0, :], ALU.mult, ALU.add)
                    link(V.scalar_tensor_tensor(phase[:, 1, k, :], sin, at_r, ptmp[:, 1, :],
                                                ALU.mult, ALU.subtract))
                V.tensor_scalar(d_col[:, 1:2], d_col[:, 0:1], 1.0 / Z_SCALE, None, ALU.mult)\
                    .then_inc(s_phase, 1)

            low_rank_a()
            ffn_stage(f_sems, 0)

            dve.wait_ge(s_phase, 1)
            dve.wait_ge(s_masked, 1)
            dve.wait_ge(s_ident, 2)
            V.scalar_tensor_tensor(toep[:, 0:P], ident[:, :], d_col[:, 1:2], toep[:, 0:P],
                                   ALU.mult, ALU.add).then_inc(s_masked, 1)
            dve.wait_ge(f_sems.x_out, SUBS)

            class Conv:
                agg, var, rstd, zs, z_used = c_agg, c_var, c_rstd, c_zs, c_tp

            def conv_ln(i):
                for b in range(2):
                    ln_stats(Conv, b, i, 2 * i + b)
                for b in range(2):
                    ln_apply(Conv, b, i, 2 * i + b)

            def conv_add(i):
                for b in range(2):
                    dve.wait_ge(c_mm[b], i + 1)
                    V.tensor_tensor(at(2 * i + b), bank[4 + b][:, :], at(2 * i + b), ALU.add)\
                        .then_inc(c_out[b], 1)

            conv_ln(0)
            with dve.Fori(1, SUBS // 2) as i:
                conv_ln(i)
                conv_add(i - 1)
            conv_add(SUBS // 2 - 1)
            for b in range(2):
                dve.wait_ge(c_out[b], SUBS // 2)
            ffn_stage(f_sems, TILES)

        @block.tensor
        def _(pe):
            mm = nc.tensor.matmul

            def x_transpose(f, b, kb, k):
                pe.wait_ge(f.z16[b], kb + 1)
                pe.wait_ge(f.xT, k)
                dst = bank[3][:, :].bitcast(F16).rearrange("p (a k t) -> p a k t", a=2, k=KH)
                for a in range(2):
                    for c in range(KH):
                        last = nc.tensor.transpose(dst[:, a, c, :], z16[:, b, a, c * P:(c + 1) * P],
                                                   ident16[:, :])
                last.then_inc(f.tp, 1)

            def p_product(f, j, k):
                pe.wait_ge(f.xT, k + 1)
                pe.wait_ge(f.p32, k)
                for c in range(KH):
                    for a in range(2):
                        last = mm(bank[2][:, 0:4 * R], xT[:, a, c, j * P:(j + 1) * P], a_w[:, c, :],
                                  start=(c == 0 and a == 0), stop=(c == KH - 1 and a == 1))
                last.then_inc(f.p_mm, 1)

            def p_transpose(f, k, pd_before):
                pe.wait_ge(f.p_stack, k + 1)
                pe.wait_ge(f.p_out, k)
                pe.wait_ge(f.pd_out, pd_before)
                for g in range(2):
                    last = nc.tensor.transpose(bank[7][:, g * P // 2:(g + 1) * P // 2].bitcast(F16),
                                               p_stack[:, g, :, :].rearrange("p a r -> p (a r)"), ident16[:, :])
                last.then_inc(f.p_t, 1)

            def ffn_stage(f, base):
                def hidden(n):
                    pe.wait_ge(f.xT, (n + 1) * TS)
                    pe.wait_ge(f.p_out, (n + 1) * TS)
                    pe.wait_ge(f.pd32, n * TS)
                    for m in range(M):
                        r, pb = rows[m], (m - 1) % 2 if m else (M - 1) % 2
                        before = uses(n, m - 1) + 1 if m else n * EVEN
                        cols = slice(m * P, m * P + r)
                        for w, wb, g, dst, dst_l, mm_s, lr_s, scaled, used in (
                                (gw, gb_w, 0, bank[0], bank[2], f.g_mm, f.gl_mm, f.tg, f.g),
                                (uw, ub_w, 1, bank[1], bank[3], f.u_mm, f.ul_mm, f.tu, f.u)):
                            pe.wait_ge(scaled[pb], before)
                            if base == 0 and g == 0:
                                chunk = sum(m >= m1 for _, m1 in CHUNKS)
                                pe.wait_ge(s_gucast, chunk + 1)
                            for c in range(KH):
                                for a in range(2):
                                    last = mm(dst[0:r, :], w[:, c, cols], xT[:, a, c, :],
                                              start=(c == 0 and a == 0), stop=(c == KH - 1 and a == 1))
                            last.then_inc(mm_s, 1)
                            pe.wait_ge(used[pb], before)
                            mm(dst_l[0:r, :], wb[:, cols], PT[:, g, :], start=True, stop=True)\
                                .then_inc(lr_s, 1)

                def down(n, j):
                    b = j % 2
                    pe.wait_ge(f.d_read[b], n * 2 + j // 2)
                    if j < 2:
                        pe.wait_ge((f.tg, f.tu)[j][(M - 1) % 2], uses(n, M - 1) + 1)
                    else:
                        pe.wait_ge(f.pd32, n * TS + j - 1)
                    for m in range(M):
                        if j == 0 and m == 0:
                            pe.wait_ge(f.hlo[0], uses(n, M - 3) + 1)
                            pe.wait_ge(f.hlo[1], uses(n, M - 4) + 1)
                        if j == 0 and m >= M - 2:
                            pe.wait_ge(f.hlo[m % 2], uses(n, m) + 1)
                        if base == 0 and j == 0:
                            pe.wait_ge(s_dcast, m + 1)
                        r = rows[m]
                        for a in range(2):
                            first, final = m == 0 and a == 0, m == M - 1 and a == 1
                            h = hT[0:r, m, a, j * P:(j + 1) * P]
                            mm(bank[4 + b][:, :], h, dw[0:r, m, :], start=first, stop=final)
                            last = mm(bank[b][:, 0:2 * R], h, da_w[0:r, m, :], start=first, stop=final)
                    last.then_inc(f.d_mm[b], 1)

                def pd_transpose(n, j, p_before):
                    pe.wait_ge(f.pd_stack, n * TS + j + 1)
                    pe.wait_ge(f.pd_out, n * TS + j)
                    pe.wait_ge(f.p_out, p_before)
                    nc.tensor.transpose(bank[7][:, 0:P // 2].bitcast(F16),
                                        pd_stack[:, :, :].rearrange("p a r -> p (a r)"), ident16[:, :])\
                        .then_inc(f.pd_t, 1)

                def down_low(n, j):
                    pe.wait_ge(f.pd_out, n * TS + j + 1)
                    pe.wait_ge(f.dsum, n * TS + j)
                    mm(bank[6][:, :], PdT[:, :], db_w[:, :], start=True, stop=True).then_inc(f.dl_mm, 1)

                def tile(n, more):
                    hidden(n)
                    k0 = (n + 1) * TS
                    for j in range(TS + 2):
                        if j < TS:
                            down(n, j)
                            if more:
                                x_transpose(f, j % 2, (n + 1) * 2 + j // 2, k0 + j)
                        if 1 <= j <= TS:
                            pd_transpose(n, j - 1, k0 + (max(0, j - 2) if more else 0))
                            if more:
                                p_product(f, j - 1, k0 + j - 1)
                            down_low(n, j - 1)
                        if more and j >= 2:
                            p_transpose(f, k0 + j - 2, n * TS + min(j, TS))

                k0 = base * TS
                for j in range(TS + 2):
                    if j < TS:
                        x_transpose(f, j % 2, base * 2 + j // 2, k0 + j)
                    if 1 <= j <= TS:
                        if base == 0 and j == 1:
                            pe.wait_ge(s_aw, 1)
                        p_product(f, j - 1, k0 + j - 1)
                    if j >= 2:
                        p_transpose(f, k0 + j - 2, k0)
                if base == 0:
                    cauchy()
                    pe.wait_ge(s_lrw, 5)
                if base == 0:
                    tile(0, True)
                with pe.Fori(max(base, 1), base + TILES - 1) as n:
                    tile(n, True)
                if base == 0:
                    toeplitz()
                tile(base + TILES - 1, False)

            def cauchy():
                pe.wait_ge(s_k, S4_RESOLVENT_STEPS)
                for k in range(KH):
                    cols = slice(8 * k, 8 * k + 8)
                    mm(bank[5][:, cols], res[:, 0, k * P:(k + 1) * P], w1[:, :], start=True, stop=False)
                    last = mm(bank[5][:, cols], res[:, 1, k * P:(k + 1) * P], w2[:, :], start=False, stop=True)
                last.then_inc(s_cauchy, 1)

            def toeplitz():
                pe.wait_ge(s_phase, 1)
                pe.wait_ge(f_sems.dsum, (TILES - 1) * TS)
                for k in range(KH):
                    for c in range(2):
                        last = mm(bank[6][:, :], phase[:, c, k, :], tab[:, c, k, :],
                                  start=(k == 0 and c == 0), stop=(k == KH - 1 and c == 1))
                last.then_inc(s_toep, 1)

            pe.wait_ge(s_kin, 160)
            for c in range(2):
                last = mm(bank[4][0:NS, c:c + 1], vct[:, c, :], bp[:, :], start=True, stop=True)
            last.then_inc(s_bmm, 1)
            pe.wait_ge(s_ident, 2)
            ffn_stage(f_sems, 0)

            pe.wait_ge(s_masked, 2)

            def conv_pair(i):
                for b in range(2):
                    pe.wait_ge(c_zs[b], i + 1)
                    pe.wait_ge(c_zT[b], i)
                    for c in range(KH):
                        last = nc.tensor.transpose(bank[b][:, c * P:(c + 1) * P],
                                                   zs[:, b, c * P:(c + 1) * P], ident[:, :])
                    last.then_inc(c_tp[b], 1)
                for b in range(2):
                    pe.wait_ge(c_zT[b], i + 1)
                    pe.wait_ge(c_out[b], i)
                    for c in range(KH):
                        last = mm(bank[4 + b][:, c * P:L], zT[:, b, c, :], toep[:, 0:L - c * P],
                                  start=(c == 0), stop=(c == KH - 1))
                    last.then_inc(c_mm[b], 1)

            conv_pair(0)
            with pe.Fori(1, SUBS // 2) as i:
                conv_pair(i)
            ffn_stage(f_sems, TILES)


_OUT = ((2, 1024, 512), "float32")


def kernel(**inputs):
    import numpy as _np
    import concourse.bacc as _bacc
    from concourse import mybir as _mybir
    from concourse.bass_utils import run_bass_kernel_spmd as _run

    a = {k: _np.asarray(v) for k, v in inputs.items()}
    H = a["L0_attn_u"].shape[-1]
    I = a["L0_ffn_gate_q"].shape[0]
    M = -(-I // P)

    def columns(v):
        padded = _np.zeros(M * P, v.dtype)
        padded[:I] = v
        return padded.reshape(M, P).T

    k = _np.arange(H, dtype=_np.float64)
    w = _np.exp(-2j * _np.pi * k / H)
    omega = _np.concatenate([1 - w.real, 1 + w.real, w.imag]).astype(_np.float32)
    opk = _np.stack([1 + w.real, w.imag]).reshape(2, H // P, P).transpose(2, 0, 1).astype(_np.float32)
    angle = 2 * _np.pi * (_np.outer(_np.arange(H), _np.arange(H)) % H) / H
    tab = _np.stack([_np.cos(angle), _np.sin(angle)]).astype(_np.float32)

    data = [
        ("x", a["L0_attn_u"].reshape(-1, H)),
        ("lambda", a["L0_attn_Lambda_ri"]), ("p", a["L0_attn_p_ri"]), ("q", a["L0_attn_q_ri"]),
        ("vc_t", a["L0_attn_Vc_ri"].transpose(2, 1, 0)), ("ct", a["L0_attn_Ct_ri"][0]),
        ("bp", a["L0_attn_Bp"]), ("d", a["L0_attn_D"]), ("log_step", a["L0_attn_log_step"]),
        ("gate_q_t", a["L0_ffn_gate_q"].T), ("gate_scale", columns(a["L0_ffn_gate_scale"])),
        ("gate_a", a["L0_ffn_gate_A"]), ("gate_b", a["L0_ffn_gate_B"]),
        ("up_q_t", a["L0_ffn_up_q"].T), ("up_scale", columns(a["L0_ffn_up_scale"])),
        ("up_a", a["L0_ffn_up_A"]), ("up_b", a["L0_ffn_up_B"]),
        ("down_q_t", a["L0_ffn_down_q"].T), ("down_scale", a["L0_ffn_down_scale"]),
        ("down_a", a["L0_ffn_down_A"]), ("down_b", a["L0_ffn_down_B"]),
        ("omega", omega), ("one_plus_omega", opk), ("tables", tab),
    ]
    nc = _bacc.Bacc("TRN2", target_bir_lowering=False, num_devices=1)
    arrays, args = {}, []
    for name, v in data:
        v = _np.ascontiguousarray(v)
        arrays[f"in_{name}"] = v
        args.append(nc.dram_tensor(f"in_{name}", v.shape, _mybir.dt.from_np(v.dtype), kind="ExternalInput").ap())
    shape, dtype = _OUT
    out = nc.dram_tensor("out_x", (shape[0] * shape[1], shape[2]), _mybir.dt.from_np(_np.dtype(dtype)),
                         kind="ExternalOutput").ap()
    s4_macaron(nc, *args, out)
    r = _run(nc, [arrays], core_ids=[0])
    return r.results[0]["out_x"].reshape(shape)
```

```python
from contextlib import ExitStack

import concourse.bass as bass
from concourse import mybir

ALU = mybir.AluOpType
ACT = mybir.ActivationFunctionType
F32, F16, I32 = mybir.dt.float32, mybir.dt.float16, mybir.dt.int32

P = 128
Q_ZERO, Q_STEP, LR_SCALE, EPS = 7.5, 0.005, 0.02, 1e-5
Z_SCALE = 2.0 ** 11
A_SCALE = B_SCALE = 2.0 ** 8
P_SCALE = 2.0 ** 4
H_SCALE = 2.0 ** 2
CHUNKS = [(0, 2), (2, 5), (5, 8), (8, 11)]


def s4_macaron(nc, x_d, lam_d, p_d, q_d, vct_d, ct_d, bp_d, dd_d, ls_d,
               gq_d, gs_d, ga_d, gb_d, uq_d, us_d, ua_d, ub_d, dq_d, ds_d, da_d, db_d,
               omega_d, opk_d, tab_d, out_d):
    T, H = x_d.shape
    I = gq_d.shape[1]
    R = ga_d.shape[1]
    NS = lam_d.shape[0]
    KH = H // P
    M = -(-I // P)
    LAST = I - (M - 1) * P
    SUBS = T // P
    TILES = T // 512
    TS = 4
    L = H
    rows = [P] * (M - 1) + [LAST]
    EVEN, ODD = (M + 1) // 2, M // 2
    x_v = x_d.rearrange("(s p) h -> p s h", p=P)
    out_v = out_d.rearrange("(s p) h -> p s h", p=P)

    def uses(n, m):
        return n * (EVEN if m % 2 == 0 else ODD) + m // 2

    with ExitStack() as ctx:
        def sb(name, shape, dt=F32):
            return ctx.enter_context(nc.sbuf_tensor(name, shape, dt))

        def sem(name):
            return ctx.enter_context(nc.semaphore(name))

        bank = [ctx.enter_context(nc.psum_tensor(f"bank{i}", [P, 512], F32)) for i in range(8)]

        X = sb("X", [P, SUBS, H])
        gq_raw = sb("gq_raw", [P, KH, I], I32)
        uq_raw = sb("uq_raw", [P, KH, I], I32)
        DQ = (M + 1) // 2
        dq_raw = sb("dq_raw", [P, DQ, H], I32)
        gw = sb("gw", [P, KH, I], F16)
        uw = sb("uw", [P, KH, I], F16)
        dw = sb("dw", [P, M, H], F16)
        a_w = sb("a_w", [P, KH, 4 * R], F16)
        da_w = sb("da_w", [P, M, 2 * R], F16)
        gb_w = sb("gb_w", [P, I], F16)
        ub_w = sb("ub_w", [P, I], F16)
        db_w = sb("db_w", [P, H], F16)
        g_scale = sb("g_scale", [P, M])
        u_scale = sb("u_scale", [P, M])
        d_scale = sb("d_scale", [P, H])
        xT = sb("xT", [P, 2, KH, 512], F16)
        PT = sb("PT", [P, 2, 512], F16)
        hT = sb("hT", [P, M, 2, 512], F16)
        stats = sb("stats", [P, 6])
        meanvar = sb("meanvar", [P, 2, 2])
        veps = sb("veps", [P, 2, 1])
        rstd = sb("rstd", [P, 2, 1])
        minus_half = sb("minus_half", [P, SUBS])
        c_stats = sb("c_stats", [P, 6])
        c_meanvar = sb("c_meanvar", [P, 2])
        c_mean = sb("c_mean", [P, SUBS])
        c_veps = sb("c_veps", [P, SUBS])
        c_rstd = sb("c_rstd", [P, SUBS])
        zs = sb("zs", [P, 2, H])
        z16 = sb("z16", [P, TS, 2, H], F16)
        p_lo = sb("p_lo", [P, 2 * R])
        p32 = sb("p32", [P, 2 * R])
        p_stack = sb("p_stack", [P, 2, 4, R], F16)
        pd_lo = sb("pd_lo", [P, R])
        pd32 = sb("pd32", [P, R])
        pd_stack = sb("pd_stack", [P, 2, 4, R], F16)
        PdT = sb("PdT", [P, P], F16)
        ident = sb("ident", [P, P])
        ident16 = sb("ident16", [P, P], F16)
        lam = sb("lam", [NS, 2])
        nlam = sb("nlam", [NS, 2])
        pv = sb("pv", [NS, 2])
        lv = sb("lv", [NS, 2, 2])
        vct = sb("vct", [NS, 2, NS])
        bp = sb("bp", [NS, 1])
        log_step = sb("log_step", [NS, 1])
        a_step = sb("a_step", [NS, 2])
        rr = sb("rr", [NS, 2, 2])
        omega_im = sb("omega_im", [NS, L])
        w1 = sb("w1", [NS, 8])
        w2 = sb("w2", [NS, 8])
        vt = sb("vt", [NS, 2, 2])
        cs = sb("cs", [P, KH, 8])
        opk = sb("opk", [P, 2, KH])
        cw = sb("cw", [P, 16, KH])
        d_col = sb("d_col", [P, 2])
        work = sb("work", [P, 12, 512])

        def parts(tensor, shapes):
            names = "pabc"[:len(tensor.shape)]
            flat = tensor[tuple(slice(0, d) for d in tensor.shape)]
            if len(tensor.shape) > 2:
                flat = flat.rearrange(f"{' '.join(names)} -> p ({' '.join(names[1:])})")
            flat = flat.bitcast(F32)
            pos, out = 0, []
            for n, *free in shapes:
                half = free[0] == "16"
                free = free[1:] if half else free
                size = 1
                for d in free:
                    size *= d
                words = size // 2 if half else size
                piece = flat[0:n, pos:pos + words]
                pos += words
                if half:
                    piece = piece.bitcast(F16)
                if len(free) > 1:
                    dims = "abc"[:len(free)]
                    piece = piece.rearrange(f"p ({' '.join(dims)}) -> p {' '.join(dims)}",
                                            **dict(zip(dims[1:], free[1:])))
                out.append(piece)
            return out

        tg, tu, g32, u32, silu, h32 = parts(work, [(P, 2, 512)] * 6)
        b_raw, db_raw, da_raw, b_hi, a_raw, db_hi = parts(
            work, [(P, 2, I), (P, H), (P, M, R), (P, "16", 2, I), (P, KH, 2 * R), (P, "16", H)])
        den, dsq, res = parts(dq_raw, [(NS, 2, L), (NS, 2, L), (NS, 2, L)])
        tab, omega_re = parts(gq_raw, [(P, 2, KH, L), (NS, 2, L)])
        phase, ptmp, toep, zT, dtmp, dsum, zc = parts(
            uq_raw, [(P, 2, KH, P), (P, 2, P), (P, L), (P, 2, KH, P), (P, 2, H), (P, H), (P, 2, H)])

        s_x = [sem(f"x_sub{j}_loaded") for j in range(TS)]
        s_xrest = sem("x_rest_loaded")
        s_q = [sem(f"gate_up_chunk{c}_loaded") for c in range(len(CHUNKS))]
        s_dq = [sem(f"down_part{c}_loaded") for c in range(2)]
        s_scale_in = sem("scales_loaded")
        s_lr = sem("low_rank_a_loaded")
        s_lrb = sem("low_rank_b_loaded")
        s_lrd = sem("low_rank_down_loaded")
        s_kin = sem("s4_inputs_loaded")
        s_tab = sem("tables_loaded")
        s_out = sem("out_stored")
        s_const = sem("constants_ready")
        s_ident = sem("identities_ready")
        s_gcast = sem("gate_cast")
        s_ucast = sem("up_cast")
        s_dcast = sem("down_cast")
        s_scales = sem("scales_ready")
        s_ahi = sem("low_rank_a_hi_ready")
        s_aw = sem("low_rank_a_ready")
        s_bhi = sem("low_rank_b_hi_ready")
        s_bw = sem("low_rank_b_ready")
        s_dhi = sem("low_rank_down_hi_ready")
        s_dw = sem("low_rank_down_ready")
        s_k = sem("dve_s4_step")
        s_bmm = sem("s4_b_mm")
        s_exp = sem("s4_step_exp")
        s_res = sem("s4_resolvents_ready")
        s_cauchy = sem("s4_cauchy_mm")
        s_phase = sem("s4_phase_ready")
        s_toep = sem("s4_toeplitz_mm")
        s_tcopy = sem("s4_toeplitz_copied")
        s_masked = sem("s4_toeplitz_masked")

        class Ffn:

            def __init__(self):
                def s(what):
                    return sem(f"ffn_{what}")

                def two(what):
                    return [s(f"{what}_{b}") for b in range(2)]

                self.agg, self.var, self.rstd = s("ln_aggregated"), s("ln_var"), s("ln_rstd")
                self.zs, self.zhi, self.z16 = s("zs"), s("z_hi"), s("z16")
                self.tp, self.xT = s("x_transposed"), s("xT_ready")
                self.p_mm, self.p_lo, self.p32 = s("p_mm"), s("p_lo"), s("p32")
                self.p_hi, self.p_stack = s("p_hi"), s("p_stack")
                self.p_t, self.p_out = s("p_transposed"), s("p_transposed_out")
                self.pd_t, self.pd_out = s("pd_transposed"), s("pd_transposed_out")
                self.g_mm, self.gl_mm, self.u_mm, self.ul_mm = s("g_mm"), s("gl_mm"), s("u_mm"), s("ul_mm")
                self.tg, self.tu, self.g, self.u = two("tg"), two("tu"), two("g"), two("u")
                self.silu, self.h, self.hhi, self.hlo = two("silu"), two("h"), two("hhi"), two("hlo")
                self.d_mm, self.d_read = two("d_mm"), two("d_read")
                self.pd_lo, self.pd32, self.pd_hi, self.pd_stack = s("pd_lo"), s("pd32"), s("pd_hi"), s("pd_stack")
                self.dl_mm, self.dsum, self.x_out = s("dl_mm"), s("dsum"), s("x_updated")

        f = Ffn()

        c_agg, c_var, c_rs = sem("conv_aggregated"), sem("conv_var"), sem("conv_rstd")
        c_z = [sem(f"conv_z_{b}") for b in range(2)]
        c_tp = [sem(f"conv_transposed_{b}") for b in range(2)]
        c_zT = [sem(f"conv_zT_{b}") for b in range(2)]
        c_mm = [sem(f"conv_mm_{b}") for b in range(2)]
        c_out = [sem(f"conv_out_{b}") for b in range(2)]
        PAIRS = SUBS // 2
        PREP = PAIRS - TS - 1

        def after(eng, semaphore, count):
            if not isinstance(count, int) or count > 0:
                eng.wait_ge(semaphore, count)

        block = ctx.enter_context(nc.Block())

        def at(s):
            return X[:, bass.ds(s, 1), :].rearrange("p a h -> p (a h)")

        @block.sync
        def _(sp):
            for j in range(TS):
                sp.dma_start(X[:, j, :], x_v[:, j, :]).then_inc(s_x[j], 16)
            gq_v = gq_d.rearrange("(k p) i -> p k i", p=P)
            uq_v = uq_d.rearrange("(k p) i -> p k i", p=P)
            for c, (m0, m1) in enumerate(CHUNKS):
                cols = slice(m0 * P, min(m1 * P, I))
                sp.dma_start(gq_raw[:, :, cols], gq_v[:, :, cols]).then_inc(s_q[c], 16)
                sp.dma_start(uq_raw[:, :, cols], uq_v[:, :, cols]).then_inc(s_q[c], 16)
            sp.dma_start(dq_raw[:, :, :],
                         dq_d[0:DQ * P, :].rearrange("(m p) h -> p m h", p=P)).then_inc(s_dq[0], 16)
            sp.dma_start(X[:, TS:SUBS, :], x_v[:, TS:SUBS, :]).then_inc(s_xrest, 16)
            sp.wait_ge(s_dcast, DQ)
            sp.dma_start(dq_raw[:, 0:M - 1 - DQ, :],
                         dq_d[DQ * P:(M - 1) * P, :].rearrange("(m p) h -> p m h", p=P)).then_inc(s_dq[1], 16)
            sp.dma_start(dq_raw[0:LAST, M - 1 - DQ, :], dq_d[(M - 1) * P:I, :]).then_inc(s_dq[1], 16)
            sp.wait_ge(s_gcast, len(CHUNKS))
            sp.dma_start(tab, tab_d.rearrange("c (k p) m -> p c k m", p=P)).then_inc(s_tab, 16)
            sp.dma_start(omega_re, omega_d[0:2, :].partition_broadcast(NS)).then_inc(s_tab, 16)

            with sp.Fori(0, SUBS) as s:
                sp.wait_ge(f.x_out, s + (SUBS + 1))
                sp.dma_start(out_v[:, bass.ds(s, 1), :], X[:, bass.ds(s, 1), :]).then_inc(s_out, 16)
            sp.wait_ge(s_out, 16 * SUBS)

        @block.gpsimd
        def _(pool):
            pool.memset(minus_half[:, :], -0.5).then_inc(s_const, 1)
            pool.memset(ident[:, :], 0.0).then_inc(s_const, 1)
            pool.memset(ident16[:, :], 0.0).then_inc(s_const, 1)
            pool.wait_ge(s_const, 3)
            for m in (ident, ident16):
                pool.affine_select(out=m[:, :], in_=m[:, :], compare_op=ALU.not_equal, fill=1.0, base=0,
                                   pattern=[[-1, P]], channel_multiplier=1).then_inc(s_ident, 1)

            def ln_rstd(k, b):
                after(pool, f.zs, k - 1)
                pool.wait_ge(f.var, k + 1)
                pool.tensor_tensor(rstd[:, b, :], veps[:, b, :], minus_half[:, 0:1], ALU.pow)\
                    .then_inc(f.rstd, 1)

            def cast_gate(c):
                cols = slice(CHUNKS[c][0] * P, min(CHUNKS[c][1] * P, I))
                pool.wait_ge(s_q[c], 32)
                pool.tensor_scalar(gw[:, :, cols], gq_raw[:, :, cols], -Q_ZERO, 1.0, ALU.add, ALU.mult)\
                    .then_inc(s_gcast, 1)

            def tiles(base):
                with pool.Fori(base + 1, base + TILES) as n:
                    for j in range(TS):
                        ln_rstd(n * TS + j, j % 2)

            for j in range(TS):
                ln_rstd(j, j % 2)
            for c in range(len(CHUNKS)):
                cast_gate(c)
            for m in range(M):
                if m in (0, DQ):
                    pool.wait_ge(s_dq[m // DQ], 16 if m == 0 else 32)
                pool.tensor_scalar(dw[0:rows[m], m, :], dq_raw[0:rows[m], m % DQ, :], -Q_ZERO, 1.0,
                                   ALU.add, ALU.mult).then_inc(s_dcast, 1)
            tiles(0)
            last = SUBS - TS - 2
            pool.wait_ge(c_var, last)
            pool.tensor_tensor(c_rstd[:, 0:last], c_veps[:, 0:last], minus_half[:, 0:last], ALU.pow)\
                .then_inc(c_rs, 1)
            pool.wait_ge(s_tcopy, 1)
            pool.affine_select(out=toep[:, 0:P], in_=toep[:, 0:P], compare_op=ALU.is_ge, fill=0.0, base=0,
                               pattern=[[1, P]], channel_multiplier=-1).then_inc(s_masked, 1)
            pool.wait_ge(c_var, SUBS)
            pool.tensor_tensor(c_rstd[:, last:SUBS], c_veps[:, last:SUBS], minus_half[:, last:SUBS], ALU.pow)\
                .then_inc(c_rs, 1)
            for j in range(TS):
                ln_rstd(SUBS + j, j % 2)
            tiles(TILES)

        @block.scalar
        def _(act):
            act.dma_start(a_raw[:, :, 0:R], ga_d.rearrange("(k p) r -> p k r", p=P)).then_inc(s_lr, 16)
            act.dma_start(a_raw[:, :, R:2 * R], ua_d.rearrange("(k p) r -> p k r", p=P)).then_inc(s_lr, 16)
            act.dma_start(g_scale[:, :], gs_d).then_inc(s_scale_in, 16)
            act.dma_start(u_scale[:, :], us_d).then_inc(s_scale_in, 16)
            for g in range(4):
                act.dma_start(b_raw[g * R:(g + 1) * R, 0, :], gb_d).then_inc(s_lrb, 16)
                act.dma_start(b_raw[g * R:(g + 1) * R, 1, :], ub_d).then_inc(s_lrb, 16)
            act.dma_start(d_scale[:, :], ds_d.partition_broadcast(P)).then_inc(s_scale_in, 16)
            for g in range(4):
                act.dma_start(db_raw[g * R:(g + 1) * R, :], db_d).then_inc(s_lrd, 16)
            act.dma_start(da_raw[:, 0:M - 1, :],
                          da_d[0:(M - 1) * P, :].rearrange("(m p) r -> p m r", p=P)).then_inc(s_lrd, 16)
            act.dma_start(da_raw[0:LAST, M - 1, :], da_d[(M - 1) * P:I, :]).then_inc(s_lrd, 16)
            act.dma_start(lam[:, :], lam_d).then_inc(s_kin, 16)
            act.dma_start(pv[:, :], p_d).then_inc(s_kin, 16)
            act.dma_start(lv[:, 0, :], ct_d).then_inc(s_kin, 16)
            act.dma_start(lv[:, 1, :], q_d).then_inc(s_kin, 16)
            act.dma_start(vct[:, :, :], vct_d.rearrange("c m n -> m c n")).then_inc(s_kin, 16)
            act.dma_start(bp[:, :], bp_d).then_inc(s_kin, 16)
            act.dma_start(log_step[:, :], ls_d.partition_broadcast(NS)).then_inc(s_kin, 16)
            act.dma_start(omega_im[:, :], omega_d[2, :].partition_broadcast(NS)).then_inc(s_kin, 16)
            act.dma_start(opk[:, :, :], opk_d).then_inc(s_kin, 16)
            act.dma_start(d_col[:, 0:1], dd_d.partition_broadcast(P)).then_inc(s_kin, 16)

            def p_low(k, bank_p):
                act.wait_ge(f.p_mm, k + 1)
                after(act, f.p32, k)
                nc.scalar.activation(p_lo[:, :], bank[bank_p][:, 2 * R:4 * R], ACT.Copy,
                                     scale=P_SCALE / (Z_SCALE * A_SCALE)).then_inc(f.p_lo, 1)

            def p_out(j, k):
                act.wait_ge(f.p_t, k + 1)
                nc.scalar.activation(PT[:, :, j * P:(j + 1) * P],
                                     bank[7][:, 0:P].bitcast(F16).rearrange("p (a t) -> p a t", a=2),
                                     ACT.Copy).then_inc(f.p_out, 1)

            def pd_low(n, j):
                b = j % 2
                act.wait_ge(f.d_mm[b], n * 2 + j // 2 + 1)
                after(act, f.pd32, n * TS + j)
                nc.scalar.activation(pd_lo[:, :], bank[b][:, R:2 * R], ACT.Copy,
                                     scale=1.0 / (H_SCALE * A_SCALE)).then_inc(f.pd_lo, 1)

            def pd_out(n, j):
                act.wait_ge(f.pd_t, n * TS + j + 1)
                after(act, f.dl_mm, n * TS + j)
                nc.scalar.activation(PdT[:, :], bank[7][:, 0:P // 2].bitcast(F16), ACT.Copy)\
                    .then_inc(f.pd_out, 1)

            def scaled(out, in_, scale, m):
                return nc.scalar.activation(out, in_, ACT.Copy, scale=scale[0:rows[m], m:m + 1])

            def h_high(n, m):
                b, r = m % 2, rows[m]
                act.wait_ge(f.h[b], uses(n, m) + 1)
                nc.scalar.activation(hT[0:r, m, 0, :], h32[0:r, b, :], ACT.Copy, scale=H_SCALE)\
                    .then_inc(f.hhi[b], 1)

            def tile(n, carry, more, s4=False):
                for m in range(M):
                    b, r, k = m % 2, rows[m], uses(n, m)
                    act.wait_ge(f.g_mm, n * M + m + 1)
                    after(act, f.g[b], k)
                    scaled(tg[0:r, b, :], bank[0][0:r, :], g_scale, m).then_inc(f.tg[b], 1)
                    if m:
                        h_high(n, m - 1)
                    act.wait_ge(f.g[b], k + 1)
                    after(act, f.h[b], k)
                    nc.scalar.activation(silu[0:r, b, :], g32[0:r, b, :], ACT.Silu).then_inc(f.silu[b], 1)
                    act.wait_ge(f.u_mm, n * M + m + 1)
                    after(act, f.u[b], k)
                    scaled(tu[0:r, b, :], bank[1][0:r, :], u_scale, m).then_inc(f.tu[b], 1)
                    if carry and m < 2:
                        pd_out(n - 1, 2 + m)
                h_high(n, M - 1)
                k0 = (n + 1) * TS
                pd_low(n, 0)
                if more:
                    p_low(k0, 2)
                pd_out(n, 0)
                if more:
                    p_low(k0 + 1, 2)
                    p_out(0, k0)
                pd_low(n, 1)
                if s4:
                    act.wait_ge(s_toep, 1)
                    nc.scalar.activation(toep[:, :], bank[2][:, :], ACT.Copy).then_inc(s_tcopy, 1)
                if more:
                    p_low(k0 + 2, 2)
                    p_out(1, k0 + 1)
                    p_low(k0 + 3, 2)
                pd_out(n, 1)
                pd_low(n, 2)
                if more:
                    p_out(2, k0 + 2)
                if s4:
                    conv_evacuate(0, 0)
                pd_low(n, 3)
                if more:
                    p_out(3, k0 + 3)
                if s4:
                    conv_evacuate(1, 0)
                if not more:
                    pd_out(n, 2)
                    pd_out(n, 3)

            def conv_evacuate(b, i):
                act.wait_ge(c_tp[b], i + 1)
                after(act, c_mm[b], i)
                nc.scalar.activation(zT[:, b, :, :], bank[2 + b][:, :].rearrange("p (k t) -> p k t", k=KH),
                                     ACT.Copy).then_inc(c_zT[b], 1)

            for j in range(TS + 1):
                if j >= 1:
                    p_low(j - 1, 2)
                if j >= 2:
                    p_out(j - 2, j - 2)
                if j == 1:
                    act.wait_ge(s_q[0], 32)
                    cols = slice(0, CHUNKS[0][1] * P)
                    nc.scalar.activation(uw[:, :, cols], uq_raw[:, :, cols], ACT.Copy, bias=-Q_ZERO)\
                        .then_inc(s_ucast, 1)
            p_out(TS - 1, TS - 1)
            act.wait_ge(s_lrb, 128)
            for g, w in enumerate((gb_w, ub_w)):
                nc.scalar.activation(w[0:2 * R, :], b_raw[0:2 * R, g, :], ACT.Copy, scale=B_SCALE)
                nc.scalar.activation(b_hi[2 * R:4 * R, g, :], b_raw[2 * R:4 * R, g, :], ACT.Copy,
                                     scale=B_SCALE).then_inc(s_bhi, 1)
            for c, (m0, m1) in list(enumerate(CHUNKS))[1:]:
                act.wait_ge(s_q[c], 32)
                cols = slice(m0 * P, min(m1 * P, I))
                nc.scalar.activation(uw[:, :, cols], uq_raw[:, :, cols], ACT.Copy, bias=-Q_ZERO)\
                    .then_inc(s_ucast, 1)
            act.wait_ge(s_kin, 160)
            nc.scalar.activation(a_step[:, 0:1], log_step[:, :], ACT.Exp, scale=-1.0).then_inc(s_exp, 1)
            act.wait_ge(s_scales, 3)
            tile(0, False, True)
            with act.Fori(1, TILES - 1) as n:
                tile(n, True, True)
            tile(TILES - 1, True, False, s4=True)
            for b in range(2):
                conv_evacuate(b, 1)
            with act.Fori(1, PREP) as i:
                for b in range(2):
                    conv_evacuate(b, i + 1)
            for i in range(PREP, PAIRS):
                q = i - PREP
                if i + 1 < PAIRS:
                    conv_evacuate(0, i + 1)
                if q:
                    p_low(SUBS + q - 1, 1)
                if i + 1 < PAIRS:
                    conv_evacuate(1, i + 1)
                if q:
                    p_out(q - 1, SUBS + q - 1)
            tile(TILES, False, True)
            with act.Fori(TILES + 1, 2 * TILES - 1) as n:
                tile(n, True, True)
            tile(2 * TILES - 1, True, False)

        @block.vector
        def _(dve):
            V = nc.vector

            def ln_stats(k, b, s):
                V.bn_stats(stats[:, :], at(s))
                dve.drain()
                V.bn_aggr(meanvar[:, b, :], stats[:, :]).then_inc(f.agg, 1)
                dve.wait_ge(f.agg, k + 1)
                V.tensor_scalar(veps[:, b, :], meanvar[:, b, 1:2], EPS, 1.0 / Z_SCALE ** 2,
                                ALU.add, ALU.mult).then_inc(f.var, 1)

            def ln_apply(k, j, s):
                b = j % 2
                after(dve, f.z16, k - 1)
                dve.wait_ge(f.rstd, k + 1)
                V.tensor_scalar(zs[:, b, :], at(s), meanvar[:, b, 0:1], rstd[:, b, :],
                                ALU.subtract, ALU.mult).then_inc(f.zs, 1)
                dve.wait_ge(f.zs, k + 1)
                after(dve, f.tp, k - TS + 1)
                V.tensor_copy(z16[:, j, 0, :], zs[:, b, :]).then_inc(f.zhi, 1)
                dve.wait_ge(f.zhi, k + 1)
                V.tensor_tensor(z16[:, j, 1, :], zs[:, b, :], z16[:, j, 0, :], ALU.subtract)\
                    .then_inc(f.z16, 1)

            def x_out(j, k, bank_t):
                dve.wait_ge(f.tp, k + 1)
                V.tensor_copy(xT[:, :, :, j * P:(j + 1) * P],
                              bank[bank_t][:, :].bitcast(F16).rearrange("p (a k t) -> p a k t", a=2, k=KH))\
                    .then_inc(f.xT, 1)

            def p_split(k, bank_p):
                dve.wait_ge(f.p_lo, k + 1)
                after(dve, f.p_stack, k)
                V.scalar_tensor_tensor(p32[:, :], bank[bank_p][:, 0:2 * R], P_SCALE / (Z_SCALE * A_SCALE),
                                       p_lo[:, :], ALU.mult, ALU.add).then_inc(f.p32, 1)
                dve.wait_ge(f.p32, k + 1)
                after(dve, f.p_t, k)
                p2 = p32[:, :].rearrange("p (g r) -> p g r", g=2)
                V.tensor_copy(p_stack[:, :, 0, :], p2)
                V.tensor_copy(p_stack[:, :, 2, :], p2).then_inc(f.p_hi, 1)
                dve.wait_ge(f.p_hi, k + 1)
                V.tensor_tensor(p_stack[:, :, 1, :], p2, p_stack[:, :, 0, :], ALU.subtract)
                V.tensor_tensor(p_stack[:, :, 3, :], p2, p_stack[:, :, 0, :], ALU.subtract)\
                    .then_inc(f.p_stack, 1)

            def h_low(n, m):
                b, r = m % 2, rows[m]
                dve.wait_ge(f.hhi[b], uses(n, m) + 1)
                V.scalar_tensor_tensor(hT[0:r, m, 1, :], h32[0:r, b, :], H_SCALE, hT[0:r, m, 0, :],
                                       ALU.mult, ALU.subtract).then_inc(f.hlo[b], 1)

            def down_read(n, j):
                b, k = j % 2, n * TS + j
                dve.wait_ge(f.pd_lo, k + 1)
                after(dve, f.pd_stack, k)
                V.scalar_tensor_tensor(pd32[:, :], bank[b][:, 0:R], 1.0 / (H_SCALE * A_SCALE),
                                       pd_lo[:, :], ALU.mult, ALU.add).then_inc(f.pd32, 1)
                dve.wait_ge(f.pd32, k + 1)
                after(dve, f.pd_t, k - 1)
                V.tensor_copy(pd_stack[:, b, 0, :], pd32[:, :])
                V.tensor_copy(pd_stack[:, b, 2, :], pd32[:, :]).then_inc(f.pd_hi, 1)
                dve.wait_ge(f.pd_hi, k + 1)
                V.tensor_tensor(pd_stack[:, b, 1, :], pd32[:, :], pd_stack[:, b, 0, :], ALU.subtract)
                V.tensor_tensor(pd_stack[:, b, 3, :], pd32[:, :], pd_stack[:, b, 0, :], ALU.subtract)\
                    .then_inc(f.pd_stack, 1)
                after(dve, f.dsum, k - 1)
                V.tensor_tensor(dtmp[:, b, :], bank[4 + b][:, :], d_scale[:, :], ALU.mult)\
                    .then_inc(f.d_read[b], 1)

            def down_add(n, j, base):
                b, k = j % 2, n * TS + j
                s = k - base * TS
                dve.wait_ge(f.dl_mm, k + 1)
                after(dve, f.x_out, k)
                dve.wait_ge(f.d_read[b], n * 2 + j // 2 + 1)
                V.scalar_tensor_tensor(dsum[:, :], bank[6][:, :], 0.5 * LR_SCALE / B_SCALE,
                                       dtmp[:, b, :], ALU.mult, ALU.add).then_inc(f.dsum, 1)
                dve.wait_ge(f.dsum, k + 1)
                V.tensor_tensor(at(s), at(s), dsum[:, :], ALU.add).then_inc(f.x_out, 1)
                if base == 0:
                    dve.drain()
                    V.bn_stats(c_stats[:, :], at(s))
                    dve.drain()
                    V.bn_aggr(c_meanvar[:, :], c_stats[:, :]).then_inc(c_agg, 1)
                    dve.wait_ge(c_agg, s + 1)
                    V.tensor_copy(c_mean[:, bass.ds(s, 1)], c_meanvar[:, 0:1])
                    V.tensor_scalar(c_veps[:, bass.ds(s, 1)], c_meanvar[:, 1:2], EPS, 1.0 / Z_SCALE ** 2,
                                    ALU.add, ALU.mult).then_inc(c_var, 1)

            def tile(n, base, carry, more, s4=False):
                c = LR_SCALE / (P_SCALE * B_SCALE)
                k0 = (n + 1) * TS
                x0 = k0 - base * TS
                for m in range(M):
                    b, r, k = m % 2, rows[m], uses(n, m)
                    dve.wait_ge(f.tg[b], k + 1)
                    dve.wait_ge(f.gl_mm, n * M + m + 1)
                    after(dve, f.silu[b], k)
                    V.scalar_tensor_tensor(g32[0:r, b, :], bank[2][0:r, :], c, tg[0:r, b, :],
                                           ALU.mult, ALU.add).then_inc(f.g[b], 1)
                    if m:
                        h_low(n, m - 1)
                    dve.wait_ge(f.tu[b], k + 1)
                    dve.wait_ge(f.ul_mm, n * M + m + 1)
                    after(dve, f.h[b], k)
                    V.scalar_tensor_tensor(u32[0:r, b, :], bank[3][0:r, :], c, tu[0:r, b, :],
                                           ALU.mult, ALU.add).then_inc(f.u[b], 1)
                    dve.wait_ge(f.u[b], k + 1)
                    dve.wait_ge(f.silu[b], k + 1)
                    after(dve, f.hlo[b], k)
                    V.tensor_tensor(h32[0:r, b, :], silu[0:r, b, :], u32[0:r, b, :], ALU.mult)\
                        .then_inc(f.h[b], 1)
                    if carry and m in (2, 3):
                        down_add(n - 1, m, base)
                    if more and m in (1, 5, 7, 9):
                        j = (1, 5, 7, 9).index(m)
                        ln_stats(k0 + j, j % 2, x0 + j)
                    if more and m in (4, 6, 8):
                        j = (4, 6, 8).index(m)
                        ln_apply(k0 + j, j, x0 + j)
                    if s4:
                        if m == 0:
                            s4_vectors()
                        if m == 1:
                            s4_den_real()
                        if m == 4:
                            s4_den_imag()
                        if m == 5:
                            s4_norm()
                        if m == 6:
                            s4_inverse()
                        if m == 7:
                            s4_resolvents()
                        if m == 8:
                            s4_sums()
                        if m == 9:
                            s4_roots()
                h_low(n, M - 1)
                if more:
                    x_out(0, k0, 3)
                    ln_apply(k0 + 3, 3, x0 + 3)
                    x_out(1, k0 + 1, 3)
                if s4:
                    s4_phase()
                down_read(n, 0)
                if more:
                    x_out(2, k0 + 2, 3)
                    p_split(k0, 2)
                    x_out(3, k0 + 3, 3)
                    p_split(k0 + 1, 2)
                down_read(n, 1)
                if more:
                    p_split(k0 + 2, 2)
                down_add(n, 0, base)
                if more:
                    p_split(k0 + 3, 2)
                if s4:
                    conv_z(0, 0)
                    conv_z(1, 0)
                down_read(n, 2)
                down_add(n, 1, base)
                if s4:
                    s4_diagonal()
                down_read(n, 3)

            def low_rank_a():
                dve.wait_ge(s_lr, 32)
                V.tensor_scalar(a_w[:, :, 0:2 * R], a_raw[:, :, :], A_SCALE, None, ALU.mult).then_inc(s_ahi, 1)
                dve.wait_ge(s_ahi, 1)
                V.scalar_tensor_tensor(a_w[:, :, 2 * R:4 * R], a_raw[:, :, :], A_SCALE, a_w[:, :, 0:2 * R],
                                       ALU.mult, ALU.subtract).then_inc(s_aw, 1)

            def low_rank_b():
                for g, w in enumerate((gb_w, ub_w)):
                    dve.wait_ge(s_bhi, g + 1)
                    V.scalar_tensor_tensor(w[2 * R:4 * R, :], b_raw[2 * R:4 * R, g, :], B_SCALE,
                                           b_hi[2 * R:4 * R, g, :], ALU.mult, ALU.subtract).then_inc(s_bw, 1)
                dve.wait_ge(s_scale_in, 48)
                for t, c in ((g_scale, Q_STEP / Z_SCALE), (u_scale, Q_STEP / Z_SCALE),
                             (d_scale, 0.5 * Q_STEP / H_SCALE)):
                    V.tensor_scalar(t[:, :], t[:, :], c, None, ALU.mult).then_inc(s_scales, 1)
                dve.wait_ge(s_scales, 3)

            def low_rank_down():
                dve.wait_ge(s_lrd, 96)
                whole, short = (slice(0, P), slice(0, M - 1)), (slice(0, LAST), slice(M - 1, M))
                V.tensor_scalar(db_w[0:2 * R, :], db_raw[0:2 * R, :], B_SCALE, None, ALU.mult)
                V.tensor_scalar(db_hi[2 * R:4 * R, :], db_raw[2 * R:4 * R, :], B_SCALE, None, ALU.mult)
                for p, m in (whole, short):
                    V.tensor_scalar(da_w[p, m, 0:R], da_raw[p, m, :], A_SCALE, None, ALU.mult).then_inc(s_dhi, 1)
                dve.wait_ge(s_dhi, 2)
                V.scalar_tensor_tensor(db_w[2 * R:4 * R, :], db_raw[2 * R:4 * R, :], B_SCALE,
                                       db_hi[2 * R:4 * R, :], ALU.mult, ALU.subtract)
                for p, m in (whole, short):
                    V.scalar_tensor_tensor(da_w[p, m, R:2 * R], da_raw[p, m, :], A_SCALE, da_w[p, m, 0:R],
                                           ALU.mult, ALU.subtract).then_inc(s_dw, 1)

            steps = [0]

            def link(ins):
                steps[0] += 1
                ins.then_inc(s_k, 1)
                dve.wait_ge(s_k, steps[0])

            def s4_vectors():
                dve.wait_ge(s_kin, 160)
                dve.wait_ge(s_bmm, 1)
                V.tensor_copy(rr[:, :, 0], bank[4][0:NS, 0:2])
                V.tensor_copy(rr[:, :, 1], pv[:, :])
                link(V.tensor_scalar(nlam[:, :], lam[:, :], -1.0, None, ALU.mult))
                for i in range(2):
                    lr, li = lv[:, i, 0:1], lv[:, i, 1:2]
                    V.tensor_scalar(vt[:, 0, :], rr[:, 1, :], li, None, ALU.mult)
                    link(V.tensor_scalar(vt[:, 1, :], rr[:, 0, :], li, None, ALU.mult))
                    V.scalar_tensor_tensor(w1[:, 2 * i:2 * i + 2], rr[:, 0, :], lr, vt[:, 0, :],
                                           ALU.mult, ALU.add)
                    link(V.scalar_tensor_tensor(w1[:, 4 + 2 * i:6 + 2 * i], rr[:, 1, :], lr, vt[:, 1, :],
                                                ALU.mult, ALU.subtract))
                V.tensor_scalar(w2[:, 0:4], w1[:, 4:8], -1.0, None, ALU.mult)
                V.tensor_copy(w2[:, 4:8], w1[:, 0:4])
                dve.wait_ge(s_exp, 1)
                link(V.tensor_scalar(a_step[:, 1:2], a_step[:, 0:1], 2.0, None, ALU.mult))

            def s4_den_real():
                dve.wait_ge(s_tab, 32)
                dve.wait_ge(s_dcast, M)
                link(V.tensor_scalar(den[:, 0, :], omega_re[:, 0, :], a_step[:, 1:2], None, ALU.mult))
                link(V.scalar_tensor_tensor(dsq[:, 0, :], omega_re[:, 1, :], nlam[:, 0:1], den[:, 0, :],
                                            ALU.mult, ALU.add))
                V.scalar_tensor_tensor(den[:, 0, :], omega_im[:, :], lam[:, 1:2], dsq[:, 0, :],
                                       ALU.mult, ALU.add)
                link(V.tensor_tensor(a_step[:, 0:1], nlam[:, 0:1], a_step[:, 1:2], ALU.subtract))

            def s4_den_imag():
                link(V.tensor_scalar(dsq[:, 1, :], omega_im[:, :], a_step[:, 0:1], None, ALU.mult))
                link(V.scalar_tensor_tensor(den[:, 1, :], omega_re[:, 1, :], nlam[:, 1:2], dsq[:, 1, :],
                                            ALU.mult, ALU.add))

            def s4_norm():
                V.tensor_tensor(dsq[:, 0, :], den[:, 0, :], den[:, 0, :], ALU.mult)
                link(V.tensor_tensor(dsq[:, 1, :], den[:, 1, :], den[:, 1, :], ALU.mult))

            def s4_inverse():
                link(V.tensor_tensor(dsq[:, 0, :], dsq[:, 0, :], dsq[:, 1, :], ALU.add))
                link(V.reciprocal(dsq[:, 1, :], dsq[:, 0, :]))

            def s4_resolvents():
                V.tensor_tensor(res[:, 0, :], den[:, 0, :], dsq[:, 1, :], ALU.mult)
                V.scalar_tensor_tensor(res[:, 1, :], den[:, 1, :], -1.0, dsq[:, 1, :],
                                       ALU.mult, ALU.mult).then_inc(s_res, 1)

            def product(o, ar, ai, br, bi):
                V.tensor_tensor(cw[:, 12, :], ar, br, ALU.mult)
                V.tensor_tensor(cw[:, 13, :], ai, bi, ALU.mult)
                V.tensor_tensor(cw[:, 14, :], ar, bi, ALU.mult)
                link(V.tensor_tensor(cw[:, 15, :], ai, br, ALU.mult))
                V.tensor_tensor(cw[:, o, :], cw[:, 12, :], cw[:, 13, :], ALU.subtract)
                link(V.tensor_tensor(cw[:, o + 1, :], cw[:, 14, :], cw[:, 15, :], ALU.add))

            def s4_sums():
                dve.wait_ge(s_cauchy, 1)
                link(V.tensor_copy(cs[:, :, :], bank[5][:, 0:8 * KH].rearrange("p (k c) -> p k c", c=8)))
                product(0, cs[:, :, 1], cs[:, :, 5], cs[:, :, 2], cs[:, :, 6])
                product(2, opk[:, 0, :], opk[:, 1, :], cw[:, 0, :], cw[:, 1, :])
                product(4, opk[:, 0, :], opk[:, 1, :], cs[:, :, 3], cs[:, :, 7])
                link(V.tensor_scalar(cw[:, 4, :], cw[:, 4, :], 1.0, None, ALU.add))

            def s4_roots():
                V.tensor_tensor(cw[:, 6, :], cw[:, 4, :], cw[:, 4, :], ALU.mult)
                link(V.tensor_tensor(cw[:, 7, :], cw[:, 5, :], cw[:, 5, :], ALU.mult))
                link(V.tensor_tensor(cw[:, 6, :], cw[:, 6, :], cw[:, 7, :], ALU.add))
                link(V.reciprocal(cw[:, 7, :], cw[:, 6, :]))
                V.tensor_tensor(cw[:, 8, :], cw[:, 4, :], cw[:, 7, :], ALU.mult)
                link(V.scalar_tensor_tensor(cw[:, 9, :], cw[:, 5, :], -1.0, cw[:, 7, :],
                                            ALU.mult, ALU.mult))
                product(10, cw[:, 2, :], cw[:, 3, :], cw[:, 8, :], cw[:, 9, :])
                V.tensor_tensor(cw[:, 0, :], cs[:, :, 0], cw[:, 10, :], ALU.subtract)
                link(V.tensor_tensor(cw[:, 1, :], cs[:, :, 4], cw[:, 11, :], ALU.subtract))
                link(V.tensor_scalar(cw[:, 2:4, :], cw[:, 0:2, :], 2.0 / (L * Z_SCALE), None, ALU.mult))

            def s4_phase():
                dve.wait_ge(s_tab, 32)
                for k in range(KH):
                    at_r, at_i = cw[:, 2, k:k + 1], cw[:, 3, k:k + 1]
                    cos, sin = tab[:, 0, k, 0:P], tab[:, 1, k, 0:P]
                    V.tensor_scalar(ptmp[:, 0, :], sin, at_i, None, ALU.mult)
                    link(V.tensor_scalar(ptmp[:, 1, :], cos, at_i, None, ALU.mult))
                    V.scalar_tensor_tensor(phase[:, 0, k, :], cos, at_r, ptmp[:, 0, :], ALU.mult, ALU.add)
                    link(V.scalar_tensor_tensor(phase[:, 1, k, :], sin, at_r, ptmp[:, 1, :],
                                                ALU.mult, ALU.subtract))
                V.tensor_scalar(d_col[:, 1:2], d_col[:, 0:1], 1.0 / Z_SCALE, None, ALU.mult)\
                    .then_inc(s_phase, 1)

            def s4_diagonal():
                dve.wait_ge(s_phase, 1)
                dve.wait_ge(s_masked, 1)
                dve.wait_ge(s_ident, 2)
                V.scalar_tensor_tensor(toep[:, 0:P], ident[:, :], d_col[:, 1:2], toep[:, 0:P],
                                       ALU.mult, ALU.add).then_inc(s_masked, 1)

            def conv_z(b, i):
                s = 2 * i + b
                after(dve, c_tp[b], i)
                V.tensor_scalar(zc[:, b, :], at(s), c_mean[:, bass.ds(s, 1)], c_rstd[:, bass.ds(s, 1)],
                                ALU.subtract, ALU.mult).then_inc(c_z[b], 1)

            def conv_add(b, i):
                dve.wait_ge(c_mm[b], i + 1)
                V.tensor_tensor(at(2 * i + b), bank[4 + b][:, :], at(2 * i + b), ALU.add)\
                    .then_inc(c_out[b], 1)

            for j in range(TS + 2):
                if j < TS:
                    dve.wait_ge(s_x[j], 16)
                    ln_stats(j, j % 2, j)
                if j == 1:
                    low_rank_a()
                if 1 <= j <= TS:
                    ln_apply(j - 1, j - 1, j - 1)
                if j >= 2:
                    x_out(j - 2, j - 2, 3)
                if j >= 3:
                    p_split(j - 3, 2)
            p_split(TS - 1, 2)
            low_rank_b()
            low_rank_down()
            dve.wait_ge(s_xrest, 16)
            tile(0, 0, False, True)
            with dve.Fori(1, TILES - 1) as n:
                tile(n, 0, True, True)
            dve.wait_ge(c_rs, 1)
            tile(TILES - 1, 0, True, False, s4=True)

            for b in range(2):
                conv_z(b, 1)
                down_add(TILES - 1, 2 + b, 0)
            for b in range(2):
                conv_add(b, 0)
            with dve.Fori(1, PREP) as i:
                for b in range(2):
                    conv_z(b, i + 1)
                for b in range(2):
                    conv_add(b, i)
            dve.wait_ge(c_rs, 2)
            for i in range(PREP, PAIRS):
                q = i - PREP
                if q:
                    x_out(q - 1, SUBS + q - 1, 0)
                if i + 1 < PAIRS:
                    for b in range(2):
                        conv_z(b, i + 1)
                if q < TS:
                    dve.wait_ge(c_out[q % 2], q // 2 + 1)
                    ln_stats(SUBS + q, q % 2, q)
                conv_add(0, i)
                if q:
                    p_split(SUBS + q - 1, 1)
                if q < TS:
                    ln_apply(SUBS + q, q, q)
                conv_add(1, i)
            for b in range(2):
                dve.wait_ge(c_out[b], PAIRS)
            tile(TILES, TILES, False, True)
            with dve.Fori(TILES + 1, 2 * TILES - 1) as n:
                tile(n, TILES, True, True)
            tile(2 * TILES - 1, TILES, True, False)
            for j in (2, 3):
                down_add(2 * TILES - 1, j, TILES)

        @block.tensor
        def _(pe):
            mm = nc.tensor.matmul

            def x_transpose(j, k, bank_t):
                pe.wait_ge(f.z16, k + 1)
                after(pe, f.xT, k)
                dst = bank[bank_t][:, :].bitcast(F16).rearrange("p (a k t) -> p a k t", a=2, k=KH)
                for a in range(2):
                    for c in range(KH):
                        last = nc.tensor.transpose(dst[:, a, c, :], z16[:, j, a, c * P:(c + 1) * P],
                                                   ident16[:, :])
                last.then_inc(f.tp, 1)

            def p_product(j, k, bank_p):
                pe.wait_ge(f.xT, k + 1)
                after(pe, f.p32, k)
                for c in range(KH):
                    for a in range(2):
                        last = mm(bank[bank_p][:, 0:4 * R], xT[:, a, c, j * P:(j + 1) * P], a_w[:, c, :],
                                  start=(c == 0 and a == 0), stop=(c == KH - 1 and a == 1))
                last.then_inc(f.p_mm, 1)

            def p_transpose(k, pd_before):
                pe.wait_ge(f.p_stack, k + 1)
                after(pe, f.p_out, k)
                after(pe, f.pd_out, pd_before)
                for g in range(2):
                    last = nc.tensor.transpose(bank[7][:, g * P // 2:(g + 1) * P // 2].bitcast(F16),
                                               p_stack[:, g, :, :].rearrange("p a r -> p (a r)"), ident16[:, :])
                last.then_inc(f.p_t, 1)

            def pd_transpose(n, j, p_before):
                pe.wait_ge(f.pd_stack, n * TS + j + 1)
                after(pe, f.pd_out, n * TS + j)
                pe.wait_ge(f.p_out, p_before)
                nc.tensor.transpose(bank[7][:, 0:P // 2].bitcast(F16),
                                    pd_stack[:, j % 2, :, :].rearrange("p a r -> p (a r)"), ident16[:, :])\
                    .then_inc(f.pd_t, 1)

            def down_low(n, j):
                pe.wait_ge(f.pd_out, n * TS + j + 1)
                after(pe, f.dsum, n * TS + j)
                mm(bank[6][:, :], PdT[:, :], db_w[:, :], start=True, stop=True).then_inc(f.dl_mm, 1)

            def down_half(n, j, half):
                b = j % 2
                if half == 0:
                    after(pe, f.d_read[b], n * 2 + j // 2)
                    if j < 2:
                        pe.wait_ge((f.tg, f.tu)[j][(M - 1) % 2], uses(n, M - 1) + 1)
                    else:
                        pe.wait_ge(f.pd32, n * TS + j - 1)
                for m in (range(0, DQ), range(DQ, M))[half]:
                    if j == 0 and m == 0:
                        pe.wait_ge(f.hlo[0], uses(n, M - 3) + 1)
                        pe.wait_ge(f.hlo[1], uses(n, M - 4) + 1)
                    if j == 0 and m >= M - 2:
                        pe.wait_ge(f.hlo[m % 2], uses(n, m) + 1)
                    if j == 0 and isinstance(n, int) and n == 0:
                        pe.wait_ge(s_dcast, m + 1)
                    r = rows[m]
                    for a in range(2):
                        first, final = m == 0 and a == 0, m == M - 1 and a == 1
                        h = hT[0:r, m, a, j * P:(j + 1) * P]
                        mm(bank[4 + b][:, :], h, dw[0:r, m, :], start=first, stop=final)
                        last = mm(bank[b][:, 0:2 * R], h, da_w[0:r, m, :], start=first, stop=final)
                if half:
                    last.then_inc(f.d_mm[b], 1)

            def tile(n, carry, more, s4=False):
                k0 = (n + 1) * TS
                p_done = k0
                pe.wait_ge(f.xT, k0)
                if carry:
                    pe.wait_ge(f.pd32, n * TS - 1)
                if s4:
                    pe.wait_ge(s_kin, 160)
                    pe.wait_ge(f.d_read[0], n * 2)
                    for c in range(2):
                        last = mm(bank[4][0:NS, c:c + 1], vct[:, c, :], bp[:, :], start=True, stop=True)
                    last.then_inc(s_bmm, 1)
                for m in range(M):
                    r, pb = rows[m], (m - 1) % 2 if m else (M - 1) % 2
                    before = uses(n, m - 1) + 1 if m else n * EVEN
                    cols = slice(m * P, m * P + r)
                    for w, wb, g, dst, dst_l, mm_s, lr_s, scaled, used, cast in (
                            (gw, gb_w, 0, bank[0], bank[2], f.g_mm, f.gl_mm, f.tg, f.g, s_gcast),
                            (uw, ub_w, 1, bank[1], bank[3], f.u_mm, f.ul_mm, f.tu, f.u, s_ucast)):
                        after(pe, scaled[pb], before)
                        if isinstance(n, int) and n == 0:
                            pe.wait_ge(cast, 1 + sum(m >= m1 for _, m1 in CHUNKS))
                        if m == 0 and g == 1:
                            after(pe, f.pd32, n * TS)
                        for c in range(KH):
                            for a in range(2):
                                last = mm(dst[0:r, :], w[:, c, cols], xT[:, a, c, :],
                                          start=(c == 0 and a == 0), stop=(c == KH - 1 and a == 1))
                        last.then_inc(mm_s, 1)
                        after(pe, used[pb], before)
                        if m == 0 and g == 0:
                            pe.wait_ge(f.p_out, k0)
                        if isinstance(n, int) and n == 0 and m == 0:
                            pe.wait_ge(s_bw, g + 1)
                        mm(dst_l[0:r, :], wb[:, cols], PT[:, g, :], start=True, stop=True)\
                            .then_inc(lr_s, 1)
                    if carry:
                        if m == 0:
                            pd_transpose(n - 1, 2, p_done)
                        if m == 1:
                            down_low(n - 1, 2)
                            pd_transpose(n - 1, 3, p_done)
                        if m == 2:
                            down_low(n - 1, 3)
                    if s4 and m == 8:
                        cauchy(n)
                if isinstance(n, int) and n == 0:
                    pe.wait_ge(s_dw, 2)
                down_half(n, 0, 0)
                if more:
                    pe.wait_ge(f.u[(M - 1) % 2], uses(n, M - 1) + 1)
                    x_transpose(0, k0, 3)
                down_half(n, 0, 1)
                if more:
                    x_transpose(1, k0 + 1, 3)
                down_half(n, 1, 0)
                if more:
                    x_transpose(2, k0 + 2, 3)
                    p_product(0, k0, 2)
                pd_transpose(n, 0, p_done)
                down_half(n, 1, 1)
                if more:
                    x_transpose(3, k0 + 3, 3)
                    p_product(1, k0 + 1, 2)
                    p_transpose(k0, n * TS + 1)
                if s4:
                    toeplitz(n)
                down_half(n, 2, 0)
                if more:
                    p_product(2, k0 + 2, 2)
                    p_transpose(k0 + 1, n * TS + 1)
                down_low(n, 0)
                down_half(n, 2, 1)
                if more:
                    p_product(3, k0 + 3, 2)
                pd_transpose(n, 1, k0 + 2 if more else p_done)
                down_half(n, 3, 0)
                if more:
                    p_transpose(k0 + 2, n * TS + 2)
                if s4:
                    conv_transpose(0, 0)
                down_low(n, 1)
                down_half(n, 3, 1)
                if more:
                    p_transpose(k0 + 3, n * TS + 2)
                if s4:
                    conv_transpose(1, 0)
                if not more:
                    pd_transpose(n, 2, p_done)

            def cauchy(n):
                pe.wait_ge(s_res, 1)
                pe.wait_ge(f.d_read[1], n * 2)
                for k in range(KH):
                    cols = slice(8 * k, 8 * k + 8)
                    mm(bank[5][:, cols], res[:, 0, k * P:(k + 1) * P], w1[:, :], start=True, stop=False)
                    last = mm(bank[5][:, cols], res[:, 1, k * P:(k + 1) * P], w2[:, :], start=False, stop=True)
                last.then_inc(s_cauchy, 1)

            def toeplitz(n):
                pe.wait_ge(s_phase, 1)
                for k in range(KH):
                    for c in range(2):
                        last = mm(bank[2][:, :], phase[:, c, k, :], tab[:, c, k, :],
                                  start=(k == 0 and c == 0), stop=(k == KH - 1 and c == 1))
                last.then_inc(s_toep, 1)

            def conv_transpose(b, i):
                pe.wait_ge(c_z[b], i + 1)
                after(pe, c_zT[b], i)
                if b == 0 and isinstance(i, int) and i == 0:
                    pe.wait_ge(s_tcopy, 1)
                for c in range(KH):
                    last = nc.tensor.transpose(bank[2 + b][:, c * P:(c + 1) * P],
                                               zc[:, b, c * P:(c + 1) * P], ident[:, :])
                last.then_inc(c_tp[b], 1)

            def conv_product(b, i):
                pe.wait_ge(c_zT[b], i + 1)
                if isinstance(i, int) and i == 0:
                    pe.wait_ge(f.d_read[b], 2 * TILES)
                after(pe, c_out[b], i)
                for c in range(KH):
                    last = mm(bank[4 + b][:, c * P:L], zT[:, b, c, :], toep[:, 0:L - c * P],
                              start=(c == 0), stop=(c == KH - 1))
                last.then_inc(c_mm[b], 1)

            pe.wait_ge(s_ident, 2)
            for j in range(TS + 2):
                if j < TS:
                    x_transpose(j, j, 3)
                if 1 <= j <= TS:
                    if j == 1:
                        pe.wait_ge(s_aw, 1)
                    p_product(j - 1, j - 1, 2)
                if j >= 2:
                    p_transpose(j - 2, 0)
            tile(0, False, True)
            with pe.Fori(1, TILES - 1) as n:
                tile(n, True, True)
            tile(TILES - 1, True, False, s4=True)

            last_tile = TILES - 1
            pe.wait_ge(s_masked, 2)
            conv_product(0, 0)
            down_low(last_tile, 2)
            pd_transpose(last_tile, 3, SUBS)
            conv_transpose(0, 1)
            conv_product(1, 0)
            down_low(last_tile, 3)
            conv_transpose(1, 1)
            with pe.Fori(1, PREP) as i:
                for b in range(2):
                    conv_product(b, i)
                    conv_transpose(b, i + 1)
            for i in range(PREP, PAIRS):
                q = i - PREP
                conv_product(0, i)
                if i + 1 < PAIRS:
                    conv_transpose(0, i + 1)
                if q:
                    if q == 1:
                        pe.wait_ge(f.pd32, TILES * TS)
                    p_product(q - 1, SUBS + q - 1, 1)
                conv_product(1, i)
                if i + 1 < PAIRS:
                    conv_transpose(1, i + 1)
                if q:
                    p_transpose(SUBS + q - 1, SUBS)
                if q < TS:
                    x_transpose(q, SUBS + q, 0)
            tile(TILES, False, True)
            with pe.Fori(TILES + 1, 2 * TILES - 1) as n:
                tile(n, True, True)
            last_tile = 2 * TILES - 1
            tile(last_tile, True, False)
            down_low(last_tile, 2)
            pd_transpose(last_tile, 3, 2 * SUBS)
            down_low(last_tile, 3)


_OUT = ((2, 1024, 512), "float32")


def kernel(**inputs):
    import numpy as _np
    import concourse.bacc as _bacc
    from concourse import mybir as _mybir
    from concourse.bass_utils import run_bass_kernel_spmd as _run

    a = {k: _np.asarray(v) for k, v in inputs.items()}
    H = a["L0_attn_u"].shape[-1]
    I = a["L0_ffn_gate_q"].shape[0]
    M = -(-I // P)

    def columns(v):
        padded = _np.zeros(M * P, v.dtype)
        padded[:I] = v
        return padded.reshape(M, P).T

    k = _np.arange(H, dtype=_np.float64)
    w = _np.exp(-2j * _np.pi * k / H)
    omega = _np.stack([1 - w.real, 1 + w.real, w.imag]).astype(_np.float32)
    opk = _np.stack([1 + w.real, w.imag]).reshape(2, H // P, P).transpose(2, 0, 1).astype(_np.float32)
    angle = 2 * _np.pi * (_np.outer(_np.arange(H), _np.arange(H)) % H) / H
    tab = _np.stack([_np.cos(angle), _np.sin(angle)]).astype(_np.float32)

    data = [
        ("x", a["L0_attn_u"].reshape(-1, H)),
        ("lambda", a["L0_attn_Lambda_ri"]), ("p", a["L0_attn_p_ri"]), ("q", a["L0_attn_q_ri"]),
        ("vc_t", a["L0_attn_Vc_ri"].transpose(2, 1, 0)), ("ct", a["L0_attn_Ct_ri"][0]),
        ("bp", a["L0_attn_Bp"]), ("d", a["L0_attn_D"]), ("log_step", a["L0_attn_log_step"]),
        ("gate_q_t", a["L0_ffn_gate_q"].T), ("gate_scale", columns(a["L0_ffn_gate_scale"])),
        ("gate_a", a["L0_ffn_gate_A"]), ("gate_b", a["L0_ffn_gate_B"]),
        ("up_q_t", a["L0_ffn_up_q"].T), ("up_scale", columns(a["L0_ffn_up_scale"])),
        ("up_a", a["L0_ffn_up_A"]), ("up_b", a["L0_ffn_up_B"]),
        ("down_q_t", a["L0_ffn_down_q"].T), ("down_scale", a["L0_ffn_down_scale"]),
        ("down_a", a["L0_ffn_down_A"]), ("down_b", a["L0_ffn_down_B"]),
        ("omega", omega), ("one_plus_omega", opk), ("tables", tab),
    ]
    nc = _bacc.Bacc("TRN2", target_bir_lowering=False, num_devices=1)
    arrays, args = {}, []
    for name, v in data:
        v = _np.ascontiguousarray(v)
        arrays[f"in_{name}"] = v
        args.append(nc.dram_tensor(f"in_{name}", v.shape, _mybir.dt.from_np(v.dtype), kind="ExternalInput").ap())
    shape, dtype = _OUT
    out = nc.dram_tensor("out_x", (shape[0] * shape[1], shape[2]), _mybir.dt.from_np(_np.dtype(dtype)),
                         kind="ExternalOutput").ap()
    s4_macaron(nc, *args, out)
    r = _run(nc, [arrays], core_ids=[0])
    return r.results[0]["out_x"].reshape(shape)
```

```python
from contextlib import ExitStack

import concourse.bass as bass
from concourse import mybir

ALU = mybir.AluOpType
ACT = mybir.ActivationFunctionType
F32, F16, I32 = mybir.dt.float32, mybir.dt.float16, mybir.dt.int32

P = 128
Q_ZERO, Q_STEP, LR_SCALE, EPS = 7.5, 0.005, 0.02, 1e-5
Z_SCALE = 2.0 ** 11
A_SCALE = B_SCALE = 2.0 ** 8
P_SCALE = 2.0 ** 4
H_SCALE = 2.0 ** 2
CHUNKS = [(0, 2), (2, 5), (5, 8), (8, 11)]


def s4_macaron(nc, x_d, state_d, step_d, gq_d, uq_d, dq_d, scales_d, ds_d, a_d, b_d, da_d, db_d,
               omega_d, opk_d, tab_d, out_d):
    T, H = x_d.shape
    I = gq_d.shape[1]
    R = b_d.shape[0] // 4
    NS = state_d.shape[0]
    KH = H // P
    M = -(-I // P)
    LAST = I - (M - 1) * P
    SUBS = T // P
    TILES = T // 512
    TS = 4
    L = H
    rows = [P] * (M - 1) + [LAST]
    EVEN, ODD = (M + 1) // 2, M // 2
    x_v = x_d.rearrange("(s p) h -> p s h", p=P)
    out_v = out_d.rearrange("(s p) h -> p s h", p=P)

    def uses(n, m):
        return n * (EVEN if m % 2 == 0 else ODD) + m // 2

    with ExitStack() as ctx:
        def sb(name, shape, dt=F32):
            return ctx.enter_context(nc.sbuf_tensor(name, shape, dt))

        def sem(name):
            return ctx.enter_context(nc.semaphore(name))

        bank = [ctx.enter_context(nc.psum_tensor(f"bank{i}", [P, 512], F32)) for i in range(8)]

        X = sb("X", [P, SUBS, H])
        gq_raw = sb("gq_raw", [P, KH, I], I32)
        uq_raw = sb("uq_raw", [P, KH, I], I32)
        DQ = (M + 1) // 2
        dq_raw = sb("dq_raw", [P, DQ, H], I32)
        gw = sb("gw", [P, KH, I], F16)
        uw = sb("uw", [P, KH, I], F16)
        dw = sb("dw", [P, M, H], F16)
        a_w = sb("a_w", [P, KH, 4 * R], F16)
        da_w = sb("da_w", [P, M, 4, R], F16)
        gb_w = sb("gb_w", [P, I], F16)
        ub_w = sb("ub_w", [P, I], F16)
        db_w = sb("db_w", [P, H], F16)
        scales = sb("scales", [P, 2, M])
        d_scale = sb("d_scale", [P, H])
        xT = sb("xT", [P, 2, KH, 512], F16)
        PT = sb("PT", [P, 2, 512], F16)
        PdT = sb("PdT", [P, 512], F16)
        hT = sb("hT", [P, M, 2, 512], F16)
        stats = sb("stats", [P, 6])
        meanvar = sb("meanvar", [P, TS, 2])
        veps = sb("veps", [P, TS, 1])
        rstd = sb("rstd", [P, TS, 1])
        minus_half = sb("minus_half", [P, SUBS])
        c_stats = sb("c_stats", [P, 6])
        c_meanvar = sb("c_meanvar", [P, 2])
        c_nmean = sb("c_nmean", [P, SUBS])
        c_bias = sb("c_bias", [P, SUBS])
        c_veps = sb("c_veps", [P, SUBS])
        c_rstd = sb("c_rstd", [P, SUBS])
        zs = sb("zs", [P, 2, H])
        z16 = sb("z16", [P, TS, 2, H], F16)
        p_stack = sb("p_stack", [P, 2, 2, 4, R], F16)
        ident = sb("ident", [P, P])
        ident16 = sb("ident16", [P, P], F16)
        state = sb("state", [NS, 9 + 2 * NS])
        lam, pv, lv, bp, vct = (state[:, 0:2], state[:, 2:4],
                                state[:, 4:8].rearrange("n (i c) -> n i c", i=2),
                                state[:, 8:9], state[:, 9:9 + 2 * NS].rearrange("n (c m) -> n c m", c=2))
        step_in = sb("step_in", [P, 2])
        nlam = sb("nlam", [NS, 2])
        a_step = sb("a_step", [NS, 3])
        rr = sb("rr", [NS, 2, 2])
        omega_im = sb("omega_im", [NS, L])
        w1 = sb("w1", [NS, 8])
        w2 = sb("w2", [NS, 8])
        vt = sb("vt", [NS, 2, 2])
        cs = sb("cs", [P, KH, 8])
        opk = sb("opk", [P, 2, KH])
        cw = sb("cw", [P, 16, KH])
        d_col = sb("d_col", [P, 1])
        ones = sb("ones", [1, P])
        k_max = sb("k_max", [1, 1])
        k_scale = sb("k_scale", [P, 2])
        work = sb("work", [P, 12, 512])
        raw_at = M - 2

        def parts(tensor, shapes, start=0):
            names = "pabc"[:len(tensor.shape)]
            flat = tensor[tuple(slice(start if i == 1 else 0, d) for i, d in enumerate(tensor.shape))]
            if len(tensor.shape) > 2:
                flat = flat.rearrange(f"{' '.join(names)} -> p ({' '.join(names[1:])})")
            flat = flat.bitcast(F32)
            pos, out = 0, []
            for n, *free in shapes:
                size = 1
                for d in free:
                    size *= d
                piece = flat[0:n, pos:pos + size]
                pos += size
                if len(free) > 1:
                    dims = "abc"[:len(free)]
                    piece = piece.rearrange(f"p ({' '.join(dims)}) -> p {' '.join(dims)}",
                                            **dict(zip(dims[1:], free[1:])))
                out.append(piece)
            return out

        tg, tu, g32, u32, silu, h32 = parts(work, [(P, 2, 512)] * 6)
        b_raw, a_raw = parts(work, [(P, 2, I), (P, KH, 2 * R)])
        da_raw, db_raw = parts(hT, [(P, M, R), (P, H)], start=raw_at)
        den, dsq, res = parts(dq_raw, [(NS, 2, L), (NS, 2, L), (NS, 2, L)])
        tab, omega_re = parts(gq_raw, [(P, 2, KH, L), (NS, 2, L)])
        phase, ptmp, toep, dtmp, dsum, czT_low = parts(
            uq_raw, [(P, 2, KH, P), (P, 2, P), (P, L), (P, 2, H), (P, H), (P, TS * H)])
        czs, = parts(uq_raw, [(P, 2, H)])
        cz16, toep16, czT_high = parts(gq_raw, [(P, TS * H), (P, L), (P, TS * H)])
        cz16 = cz16.bitcast(F16).rearrange("p (j a h) -> p j a h", j=TS, a=2)
        czT = [t.bitcast(F16).rearrange("p (j a k t) -> p j a k t", j=TS, a=2, k=KH)
               for t in (czT_low, czT_high)]
        toep16 = toep16.bitcast(F16).rearrange("p (a m) -> p a m", a=2)

        s_x = [sem(f"x_sub{j}_loaded") for j in range(TS)]
        s_xrest = [sem(f"x_rest_part{c}_loaded") for c in range(2)]
        s_q = [sem(f"gate_up_chunk{c}_loaded") for c in range(len(CHUNKS))]
        s_dq = [sem(f"down_part{c}_loaded") for c in range(2)]
        s_scale_in = sem("gate_up_scales_loaded")
        s_step_in = sem("log_step_and_d_loaded")
        s_lr = sem("low_rank_a_loaded")
        s_lrb = [sem(f"low_rank_b_{g}_loaded") for g in ("gate", "up")]
        s_lrd = sem("low_rank_down_loaded")
        s_kin = sem("s4_inputs_loaded")
        s_tab = sem("tables_loaded")
        s_released = sem("transpose_released")
        s_out = sem("out_stored")
        s_const = sem("constants_ready")
        s_ident = sem("identities_ready")
        s_gcast = sem("gate_cast")
        s_ucast = sem("up_cast")
        s_dcast = sem("down_cast")
        s_scales = sem("scales_ready")
        s_ahi = sem("low_rank_a_hi_ready")
        s_aw = sem("low_rank_a_ready")
        s_bhi = [sem(f"low_rank_b_{g}_hi_ready") for g in ("gate", "up")]
        s_bw = sem("low_rank_b_ready")
        s_dhi = sem("low_rank_down_hi_ready")
        s_dw = sem("low_rank_down_ready")
        s_k = sem("dve_s4_step")
        s_kp = sem("pool_s4_step")
        s_den = sem("s4_norms_ready")
        s_inverse = sem("s4_inverses_ready")
        s_bmm = sem("s4_b_mm")
        s_exp = sem("s4_step_exp")
        s_res = sem("s4_resolvents_ready")
        s_cauchy = sem("s4_cauchy_mm")
        s_phase = sem("s4_phase_ready")
        s_toep = sem("s4_toeplitz_mm")
        s_tcopy = sem("s4_toeplitz_copied")
        s_masked = sem("s4_toeplitz_masked")
        s_max = sem("s4_toeplitz_max")
        s_maxmm = sem("s4_max_everywhere")
        s_split = sem("s4_toeplitz_split")

        class Ffn:

            def __init__(self):
                def s(what):
                    return sem(f"ffn_{what}")

                def two(what):
                    return [s(f"{what}_{b}") for b in range(2)]

                self.agg, self.var, self.rstd = s("ln_aggregated"), s("ln_var"), s("ln_rstd")
                self.zs, self.zhi, self.z16 = s("zs"), s("z_hi"), s("z16")
                self.tp0, self.xT0 = s("first_x_transposed"), s("first_xT_ready")
                self.xT = [s(f"xT_sub{j}_ready") for j in range(4)]
                self.p_mm, self.p_hi, self.p_stack = s("p_mm"), s("p_hi"), s("p_stack")
                self.p_t0, self.PT0 = s("first_p_transposed"), s("first_PT_ready")
                self.PT = two("PT_ready")
                self.pd_mm, self.pd_hi, self.pd_out = s("pd_mm"), s("pd_hi"), s("pd_ready")
                self.g_mm, self.gl_mm, self.u_mm, self.ul_mm = s("g_mm"), s("gl_mm"), s("u_mm"), s("ul_mm")
                self.tg, self.tu, self.g, self.u = two("tg"), two("tu"), two("g"), two("u")
                self.silu, self.h, self.hhi, self.hlo = two("silu"), two("h"), two("hhi"), two("hlo")
                self.d_mm, self.d_read = two("d_mm"), two("d_read")
                self.dl_mm, self.dsum, self.x_out = s("dl_mm"), s("dsum"), s("x_updated")

        f = Ffn()

        c_agg, c_var, c_rs, c_nb = (sem("conv_aggregated"), sem("conv_var"), sem("conv_rstd"),
                                    sem("conv_bias"))
        c_zs, c_zhi = sem("conv_zs"), sem("conv_z_hi")
        c_z16, c_z16_rest = sem("conv_first_z16"), sem("conv_other_z16")
        c_zT = [sem(f"conv_zT_{j}_ready") for j in range(2 * TS)]
        c_mm = [sem(f"conv_mm_{j}") for j in range(TS)]
        c_out = [sem(f"conv_out_{j}") for j in range(TS)]
        c_bank = [bank[4], bank[5], bank[2], bank[3]]
        AHEAD = TS + 2
        LN_STEP = {TS - 1 + 2 * q: q for q in range(TS)}
        P_STEP = {2 * TS + 2 * q: q for q in range(TS)}

        def after(eng, semaphore, count):
            if not isinstance(count, int) or count > 0:
                eng.wait_ge(semaphore, count)

        def p_bank(n, j):
            return bank[4 + j % 3] if isinstance(n, int) and n == 0 else bank[1]

        def wait_z16(eng, i):
            if i < TS:
                eng.wait_ge(c_z16, i + 1)
            else:
                eng.wait_ge(c_z16_rest, i - TS + 1)

        block = ctx.enter_context(nc.Block())

        def at(s):
            return X[:, bass.ds(s, 1), :].rearrange("p a h -> p (a h)")

        @block.sync
        def _(sp):
            for j in range(TS):
                sp.dma_start(X[:, j, :], x_v[:, j, :]).then_inc(s_x[j], 16)
            gq_v = gq_d.rearrange("(k p) i -> p k i", p=P)
            uq_v = uq_d.rearrange("(k p) i -> p k i", p=P)
            for c, (m0, m1) in enumerate(CHUNKS):
                cols = slice(m0 * P, min(m1 * P, I))
                sp.dma_start(gq_raw[:, :, cols], gq_v[:, :, cols]).then_inc(s_q[c], 16)
                sp.dma_start(uq_raw[:, :, cols], uq_v[:, :, cols]).then_inc(s_q[c], 16)
                if c == 0:
                    for g in range(2):
                        sp.dma_start(b_raw[:, g, :], b_d[:, g, :]).then_inc(s_lrb[g], 16)
            sp.dma_start(X[:, TS:2 * TS, :], x_v[:, TS:2 * TS, :]).then_inc(s_xrest[0], 16)
            sp.dma_start(da_raw, da_d).then_inc(s_lrd, 16)
            sp.dma_start(db_raw, db_d).then_inc(s_lrd, 16)
            sp.dma_start(d_scale[:, :], ds_d.partition_broadcast(P)).then_inc(s_lrd, 16)
            sp.dma_start(dq_raw[:, :, :],
                         dq_d[0:DQ * P, :].rearrange("(m p) h -> p m h", p=P)).then_inc(s_dq[0], 16)
            sp.dma_start(state[:, :], state_d).then_inc(s_kin, 16)
            sp.dma_start(omega_im[:, :], omega_d[2, :].partition_broadcast(NS)).then_inc(s_kin, 16)
            sp.dma_start(opk[:, :, :], opk_d).then_inc(s_kin, 16)
            sp.dma_start(X[:, 2 * TS:SUBS, :], x_v[:, 2 * TS:SUBS, :]).then_inc(s_xrest[1], 16)
            sp.wait_ge(s_dcast, DQ)
            sp.dma_start(dq_raw[:, 0:M - 1 - DQ, :],
                         dq_d[DQ * P:(M - 1) * P, :].rearrange("(m p) h -> p m h", p=P)).then_inc(s_dq[1], 16)
            sp.dma_start(dq_raw[0:LAST, M - 1 - DQ, :], dq_d[(M - 1) * P:I, :]).then_inc(s_dq[1], 16)
            sp.wait_ge(s_gcast, len(CHUNKS))
            sp.dma_start(tab, tab_d.rearrange("c (k p) m -> p c k m", p=P)).then_inc(s_tab, 16)
            sp.dma_start(omega_re, omega_d[0:2, :].partition_broadcast(NS)).then_inc(s_tab, 16)

            def transpose(n, what, j):
                cols = slice(j * P, (j + 1) * P)
                if what == "x":
                    sp.wait_ge(f.z16, n * TS + j + 1)
                    sp.sem_inc(s_released, 1)
                    sp.dma_start(xT[:, :, :, cols].rearrange("p a k t -> p (a k) t"),
                                 z16[:, j, :, :].rearrange("p a h -> p (a h)"), transpose=True)\
                        .then_inc(f.xT[j], 16)
                else:
                    sp.wait_ge(f.p_stack, n * TS + j + 1)
                    sp.sem_inc(s_released, 1)
                    sp.dma_start(PT[:, :, cols], p_stack[:, j % 2, :, :, :].rearrange("p g a r -> p (g a r)"),
                                 transpose=True).then_inc(f.PT[j % 2], 16)

            def transposes(n):
                sp.wait_ge(f.ul_mm, n * M)
                for what, j in ("x", 0), ("x", 1), ("x", 2), ("p", 0), ("x", 3), ("p", 1), ("p", 2), ("p", 3):
                    transpose(n, what, j)

            def conv_transpose(i):
                wait_z16(sp, i)
                if i >= 2 * TS:
                    sp.wait_ge(c_mm[i % TS], i // TS - 1)
                sp.dma_start(czT[i // TS % 2][:, i % TS, :, :, :].rearrange("p a k t -> p (a k) t"),
                             cz16[:, i % TS, :, :].rearrange("p a h -> p (a h)"), transpose=True)\
                    .then_inc(c_zT[i % (2 * TS)], 16)

            with sp.Fori(1, TILES) as n:
                transposes(n)
            for i in range(AHEAD):
                conv_transpose(i)
            for i in range(SUBS):
                if i + AHEAD < SUBS:
                    conv_transpose(i + AHEAD)
                if i - 1 in LN_STEP:
                    transpose(TILES, "x", LN_STEP[i - 1])
                if i in P_STEP:
                    transpose(TILES, "p", P_STEP[i])
            with sp.Fori(TILES + 1, 2 * TILES) as n:
                transposes(n)
            with sp.Fori(0, SUBS) as s:
                sp.wait_ge(f.x_out, s + (SUBS + 1))
                sp.dma_start(out_v[:, bass.ds(s, 1), :], X[:, bass.ds(s, 1), :]).then_inc(s_out, 16)
            sp.wait_ge(s_out, 16 * SUBS)

        @block.gpsimd
        def _(pool):
            pool.memset(minus_half[:, :], -0.5).then_inc(s_const, 1)
            pool.memset(ones[:, :], 1.0).then_inc(s_const, 1)
            pool.memset(ident[:, :], 0.0).then_inc(s_const, 1)
            pool.memset(ident16[:, :], 0.0).then_inc(s_const, 1)
            pool.wait_ge(s_const, 4)
            for m in (ident, ident16):
                pool.affine_select(out=m[:, :], in_=m[:, :], compare_op=ALU.not_equal, fill=1.0, base=0,
                                   pattern=[[-1, P]], channel_multiplier=1).then_inc(s_ident, 1)

            def ln_rstd(k, b):
                after(pool, f.zs, k - TS + 1)
                pool.wait_ge(f.var, k + 1)
                pool.tensor_tensor(rstd[:, b, :], veps[:, b, :], minus_half[:, 0:1], ALU.pow)\
                    .then_inc(f.rstd, 1)

            def cast_gate(c):
                cols = slice(CHUNKS[c][0] * P, min(CHUNKS[c][1] * P, I))
                pool.wait_ge(s_q[c], 32)
                pool.tensor_scalar(gw[:, :, cols], gq_raw[:, :, cols], -Q_ZERO, 1.0, ALU.add, ALU.mult)\
                    .then_inc(s_gcast, 1)

            def tile_rstds(n, subs=range(TS)):
                for j in subs:
                    ln_rstd(n * TS + j, j)

            steps = [0]

            def link(ins):
                steps[0] += 1
                ins.then_inc(s_kp, 1)
                pool.wait_ge(s_kp, steps[0])

            def s4_norms_real():
                pool.wait_ge(s_kin, 48)
                pool.wait_ge(s_exp, 1)
                pool.wait_ge(s_tab, 32)
                pool.tensor_scalar(nlam[:, :], lam, -1.0, None, ALU.mult)
                link(pool.tensor_scalar(a_step[:, 1:2], a_step[:, 0:1], 2.0, None, ALU.mult))
                link(pool.tensor_tensor(a_step[:, 2:3], nlam[:, 0:1], a_step[:, 1:2], ALU.subtract))
                pool.tensor_scalar(den[:, 0, :], omega_re[:, 0, :], a_step[:, 1:2], None, ALU.mult)
                pool.tensor_scalar(dsq[:, 0, :], omega_re[:, 1, :], nlam[:, 0:1], None, ALU.mult)
                link(pool.tensor_scalar(dsq[:, 1, :], omega_im[:, :], lam[:, 1:2], None, ALU.mult))
                link(pool.tensor_tensor(den[:, 0, :], den[:, 0, :], dsq[:, 0, :], ALU.add))
                link(pool.tensor_tensor(den[:, 0, :], den[:, 0, :], dsq[:, 1, :], ALU.add))

            def s4_norms_imag():
                pool.tensor_scalar(den[:, 1, :], omega_im[:, :], a_step[:, 2:3], None, ALU.mult)
                link(pool.tensor_scalar(dsq[:, 1, :], omega_re[:, 1, :], nlam[:, 1:2], None, ALU.mult))
                link(pool.tensor_tensor(den[:, 1, :], den[:, 1, :], dsq[:, 1, :], ALU.add))
                pool.tensor_tensor(dsq[:, 0, :], den[:, 0, :], den[:, 0, :], ALU.mult)
                link(pool.tensor_tensor(dsq[:, 1, :], den[:, 1, :], den[:, 1, :], ALU.mult))
                pool.tensor_tensor(dsq[:, 0, :], dsq[:, 0, :], dsq[:, 1, :], ALU.add).then_inc(s_den, 1)

            tile_rstds(0, range(0, 3))
            cast_gate(0)
            tile_rstds(0, range(3, TS))
            pool.wait_ge(s_lrb[1], 16)
            pool.tensor_scalar(ub_w[:, :], b_raw[:, 1, :], B_SCALE, 0.0, ALU.mult, ALU.add).then_inc(s_bhi[1], 1)
            for c in range(1, len(CHUNKS)):
                cast_gate(c)
            for m in range(M):
                if m == DQ:
                    tile_rstds(1, range(0, 2))
                if m in (0, DQ):
                    pool.wait_ge(s_dq[m // DQ], 16 if m == 0 else 32)
                pool.tensor_scalar(dw[0:rows[m], m, :], dq_raw[0:rows[m], m % DQ, :], -Q_ZERO, 1.0,
                                   ALU.add, ALU.mult).then_inc(s_dcast, 1)
            tile_rstds(1, range(2, 3))
            s4_norms_real()
            tile_rstds(1, range(3, TS))
            s4_norms_imag()
            with pool.Fori(2, TILES) as n:
                tile_rstds(n)
            def conv_rstds(c, subs):
                pool.wait_ge(c_var, subs.stop)
                pool.tensor_tensor(c_rstd[:, subs], c_veps[:, subs], minus_half[:, subs], ALU.pow)\
                    .then_inc(c_rs, 1)
                pool.wait_ge(c_rs, c + 1)
                pool.tensor_tensor(c_bias[:, subs], c_nmean[:, subs], c_rstd[:, subs], ALU.mult)\
                    .then_inc(c_nb, 1)

            def conv_low(i):
                b, j = i % 2, i % TS
                pool.wait_ge(c_zhi, i + 1)
                pool.tensor_tensor(cz16[:, j, 1, :], czs[:, b, :], cz16[:, j, 0, :], ALU.subtract)\
                    .then_inc(c_z16_rest, 1)

            conv_rstds(0, slice(0, SUBS - TS))
            pool.wait_ge(s_tcopy, 1)
            pool.affine_select(out=toep[:, 0:P], in_=toep[:, 0:P], compare_op=ALU.is_ge, fill=0.0, base=0,
                               pattern=[[1, P]], channel_multiplier=-1).then_inc(s_masked, 1)
            for i in range(TS, SUBS):
                conv_low(i)
                if i == 2 * TS - 1:
                    conv_rstds(1, slice(SUBS - TS, SUBS))
                if i - TS - 1 in LN_STEP:
                    q = LN_STEP[i - TS - 1]
                    ln_rstd(SUBS + q, q)
            with pool.Fori(TILES + 1, 2 * TILES) as n:
                tile_rstds(n)

        @block.scalar
        def _(act):
            act.dma_start(step_in[:, :], step_d.partition_broadcast(P)).then_inc(s_step_in, 16)
            act.dma_start(a_raw, a_d.rearrange("(k p) r -> p k r", p=P)).then_inc(s_lr, 16)
            act.dma_start(scales[:, :, :], scales_d).then_inc(s_scale_in, 16)
            act.wait_ge(s_step_in, 16)
            nc.scalar.activation(a_step[:, 0:1], step_in[0:NS, 0:1], ACT.Exp, scale=-1.0).then_inc(s_exp, 1)

            def p_high(n, j):
                act.wait_ge(f.p_mm, n * TS + j + 1)
                if isinstance(n, int) and n * TS + j < TS + 2:
                    after(act, f.p_t0, n * TS + j - 1)
                else:
                    act.wait_ge(f.PT[j % 2], (n - 1) * 32 + j // 2 * 16)
                for slot, part in ((0, 0), (3, 0), (2, 1)):
                    last = nc.scalar.activation(
                        p_stack[:, j % 2, :, slot, :],
                        p_bank(n, j)[:, part * 2 * R:(part + 1) * 2 * R].rearrange("p (g r) -> p g r", g=2),
                        ACT.Copy, scale=P_SCALE / (Z_SCALE * A_SCALE))
                last.then_inc(f.p_hi, 1)

            def p_out(j):
                act.wait_ge(f.p_t0, j + 1)
                nc.scalar.activation(PT[:, :, j * P:(j + 1) * P],
                                     bank[7][:, 0:P].bitcast(F16).rearrange("p (a t) -> p a t", a=2),
                                     ACT.Copy).then_inc(f.PT0, 1)

            def pd_high(n):
                act.wait_ge(f.pd_mm, n + 1)
                after(act, f.dl_mm, n * TS)
                nc.scalar.activation(PdT[:, :], bank[0][:, :], ACT.Copy,
                                     scale=1.0 / (H_SCALE * A_SCALE)).then_inc(f.pd_hi, 1)

            def x_out(j, k, bank_t):
                act.wait_ge(f.tp0, k + 1)
                nc.scalar.activation(xT[:, :, :, j * P:(j + 1) * P],
                                     bank[bank_t][:, :].bitcast(F16).rearrange("p (a k t) -> p a k t", a=2, k=KH),
                                     ACT.Copy).then_inc(f.xT0, 1)

            def scaled(out, in_, g, m):
                return nc.scalar.activation(out, in_, ACT.Copy, scale=scales[0:rows[m], g, m:m + 1])

            def h_high(n, m):
                b, r = m % 2, rows[m]
                act.wait_ge(f.h[b], uses(n, m) + 1)
                nc.scalar.activation(hT[0:r, m, 0, :], h32[0:r, b, :], ACT.Copy, scale=H_SCALE)\
                    .then_inc(f.hhi[b], 1)

            def tile(n, more, s4=False):
                for m in range(M):
                    b, r, k = m % 2, rows[m], uses(n, m)
                    act.wait_ge(f.g_mm, n * M + m + 1)
                    after(act, f.g[b], k)
                    scaled(tg[0:r, b, :], bank[0][0:r, :], 0, m).then_inc(f.tg[b], 1)
                    if m:
                        h_high(n, m - 1)
                    act.wait_ge(f.u_mm, n * M + m + 1)
                    after(act, f.u[b], k)
                    scaled(tu[0:r, b, :], bank[1][0:r, :], 1, m).then_inc(f.tu[b], 1)
                    act.wait_ge(f.g[b], k + 1)
                    after(act, f.h[b], k)
                    nc.scalar.activation(silu[0:r, b, :], g32[0:r, b, :], ACT.Silu).then_inc(f.silu[b], 1)
                    if isinstance(n, int) and n == 0 and m in (0, 2, 4):
                        cast_up(1 + m // 2)
                h_high(n, M - 1)
                pd_high(n)
                if more:
                    for j in range(TS):
                        p_high(n + 1, j)
                if s4:
                    act.wait_ge(s_toep, 1)
                    nc.scalar.activation(toep[:, :], bank[2][:, :], ACT.Copy).then_inc(s_tcopy, 1)
                    for i in range(AHEAD):
                        conv_norm(i)

            def conv_norm(i):
                b, j = i % 2, i % TS
                act.wait_ge(c_nb, 1 + i // (SUBS - TS))
                if i >= 2:
                    wait_z16(act, i - 2)
                nc.scalar.activation(czs[:, b, :], X[:, i, :], ACT.Identity, bias=c_bias[:, i:i + 1],
                                     scale=c_rstd[:, i:i + 1]).then_inc(c_zs, 1)
                act.wait_ge(c_zs, i + 1)
                if i >= TS:
                    before = i - TS
                    act.wait_ge(c_zT[before % (2 * TS)], before // (2 * TS) * 16 + 16)
                nc.scalar.activation(cz16[:, j, 0, :], czs[:, b, :], ACT.Copy).then_inc(c_zhi, 1)

            def cast_up(c):
                act.wait_ge(s_q[c], 32)
                cols = slice(CHUNKS[c][0] * P, min(CHUNKS[c][1] * P, I))
                nc.scalar.activation(uw[:, :, cols], uq_raw[:, :, cols], ACT.Copy, bias=-Q_ZERO)\
                    .then_inc(s_ucast, 1)

            x_out(0, 0, 2)
            cast_up(0)
            x_out(1, 1, 3)
            act.wait_ge(s_lrb[0], 16)
            nc.scalar.activation(gb_w[:, :], b_raw[:, 0, :], ACT.Copy, scale=B_SCALE).then_inc(s_bhi[0], 1)
            x_out(2, 2, 2)
            x_out(3, 3, 3)
            p_high(0, 0)
            p_high(0, 1)
            p_out(0)
            p_high(0, 2)
            p_out(1)
            p_high(0, 3)
            p_out(2)
            p_out(3)
            act.wait_ge(s_scales, 1)
            act.wait_ge(s_bw, 2)
            tile(0, True)
            with act.Fori(1, TILES - 1) as n:
                tile(n, True)
            tile(TILES - 1, False, s4=True)
            for i in range(SUBS):
                if i + AHEAD < SUBS:
                    conv_norm(i + AHEAD)
                if i in P_STEP:
                    p_high(TILES, P_STEP[i])
            tile(TILES, True)
            with act.Fori(TILES + 1, 2 * TILES - 1) as n:
                tile(n, True)
            tile(2 * TILES - 1, False)

        @block.vector
        def _(dve):
            V = nc.vector

            def ln_stats(k, b, s):
                V.bn_stats(stats[:, :], at(s))
                dve.drain()
                V.bn_aggr(meanvar[:, b, :], stats[:, :]).then_inc(f.agg, 1)
                dve.wait_ge(f.agg, k + 1)
                V.tensor_scalar(veps[:, b, :], meanvar[:, b, 1:2], EPS, 1.0 / Z_SCALE ** 2,
                                ALU.add, ALU.mult).then_inc(f.var, 1)

            def ln_apply(n, j, s):
                b, k = j % 2, n * TS + j
                after(dve, f.z16, k - 1)
                dve.wait_ge(f.rstd, k + 1)
                V.tensor_scalar(zs[:, b, :], at(s), meanvar[:, j, 0:1], rstd[:, j, :],
                                ALU.subtract, ALU.mult).then_inc(f.zs, 1)
                dve.wait_ge(f.zs, k + 1)
                if isinstance(n, int) and n == 1:
                    dve.wait_ge(f.tp0, j + 1)
                else:
                    after(dve, f.xT[j], (n - 1) * 16)
                V.tensor_copy(z16[:, j, 0, :], zs[:, b, :]).then_inc(f.zhi, 1)
                dve.wait_ge(f.zhi, k + 1)
                V.tensor_tensor(z16[:, j, 1, :], zs[:, b, :], z16[:, j, 0, :], ALU.subtract)\
                    .then_inc(f.z16, 1)

            def p_split(n, j):
                dve.wait_ge(f.p_hi, n * TS + j + 1)
                V.scalar_tensor_tensor(p_stack[:, j % 2, :, 1, :],
                                       p_bank(n, j)[:, 0:2 * R].rearrange("p (g r) -> p g r", g=2),
                                       P_SCALE / (Z_SCALE * A_SCALE), p_stack[:, j % 2, :, 0, :],
                                       ALU.mult, ALU.subtract).then_inc(f.p_stack, 1)

            def pd_split(n):
                dve.wait_ge(f.pd_hi, n + 1)
                V.scalar_tensor_tensor(PdT[R:2 * R, :], bank[0][R:2 * R, :], 1.0 / (H_SCALE * A_SCALE),
                                       PdT[R:2 * R, :], ALU.mult, ALU.subtract).then_inc(f.pd_out, 1)

            def h_low(n, m):
                b, r = m % 2, rows[m]
                dve.wait_ge(f.hhi[b], uses(n, m) + 1)
                V.scalar_tensor_tensor(hT[0:r, m, 1, :], h32[0:r, b, :], H_SCALE, hT[0:r, m, 0, :],
                                       ALU.mult, ALU.subtract).then_inc(f.hlo[b], 1)

            def down_read(n, j):
                b, k = j % 2, n * TS + j
                dve.wait_ge(f.d_mm[b], n * 2 + j // 2 + 1)
                after(dve, f.dsum, k - 1)
                V.tensor_tensor(dtmp[:, b, :], bank[4 + b][:, :], d_scale[:, :], ALU.mult)\
                    .then_inc(f.d_read[b], 1)

            def down_add(n, j, base):
                b, k = j % 2, n * TS + j
                s = k - base * TS
                dve.wait_ge(f.dl_mm, k + 1)
                after(dve, f.x_out, k)
                dve.wait_ge(f.d_read[b], n * 2 + j // 2 + 1)
                V.scalar_tensor_tensor(dsum[:, :], bank[6][:, :], 0.5 * LR_SCALE / B_SCALE,
                                       dtmp[:, b, :], ALU.mult, ALU.add).then_inc(f.dsum, 1)
                dve.wait_ge(f.dsum, k + 1)
                V.tensor_tensor(at(s), at(s), dsum[:, :], ALU.add).then_inc(f.x_out, 1)
                if base == 0:
                    dve.drain()
                    V.bn_stats(c_stats[:, :], at(s))
                    dve.drain()
                    V.bn_aggr(c_meanvar[:, :], c_stats[:, :]).then_inc(c_agg, 1)
                    dve.wait_ge(c_agg, s + 1)
                    V.tensor_scalar(c_nmean[:, bass.ds(s, 1)], c_meanvar[:, 0:1], -1.0, None, ALU.mult)
                    V.tensor_scalar(c_veps[:, bass.ds(s, 1)], c_meanvar[:, 1:2], EPS, 1.0 / Z_SCALE ** 2,
                                    ALU.add, ALU.mult).then_inc(c_var, 1)

            def tile(n, base, more, s4=False):
                c = LR_SCALE / (P_SCALE * B_SCALE)
                k0 = (n + 1) * TS
                x0 = k0 - base * TS
                for m in range(M):
                    b, r, k = m % 2, rows[m], uses(n, m)
                    dve.wait_ge(f.tg[b], k + 1)
                    dve.wait_ge(f.gl_mm, n * M + m + 1)
                    after(dve, f.silu[b], k)
                    V.scalar_tensor_tensor(g32[0:r, b, :], bank[2][0:r, :], c, tg[0:r, b, :],
                                           ALU.mult, ALU.add).then_inc(f.g[b], 1)
                    if m:
                        h_low(n, m - 1)
                    if isinstance(n, int) and n == 0 and m == 1:
                        dve.wait_ge(s_xrest[0], 16)
                    if isinstance(n, int) and n == 0 and m == 2:
                        down_b()
                    if isinstance(n, int) and n == 0 and m == 4:
                        down_a()
                    dve.wait_ge(f.tu[b], k + 1)
                    dve.wait_ge(f.ul_mm, n * M + m + 1)
                    after(dve, f.h[b], k)
                    V.scalar_tensor_tensor(u32[0:r, b, :], bank[3][0:r, :], c, tu[0:r, b, :],
                                           ALU.mult, ALU.add).then_inc(f.u[b], 1)
                    dve.wait_ge(f.u[b], k + 1)
                    dve.wait_ge(f.silu[b], k + 1)
                    after(dve, f.hlo[b], k)
                    V.tensor_tensor(h32[0:r, b, :], silu[0:r, b, :], u32[0:r, b, :], ALU.mult)\
                        .then_inc(f.h[b], 1)
                    if more and m in (1, 3, 6, 8):
                        j = (1, 3, 6, 8).index(m)
                        ln_stats(k0 + j, j, x0 + j)
                    if more and m in (5, 7):
                        j = (5, 7).index(m)
                        ln_apply(n + 1, j, x0 + j)
                    if s4:
                        if m == 0:
                            s4_inverse(1)
                        if m == 1:
                            s4_resolvents()
                        if m == 3:
                            s4_sums()
                        if m == 4:
                            s4_roots()
                        if m in (6, 8):
                            s4_phase(m - 6, m - 4)
                h_low(n, M - 1)
                if more:
                    for j in (2, 3):
                        ln_apply(n + 1, j, x0 + j)
                pd_split(n)
                if more:
                    p_split(n + 1, 0)
                    p_split(n + 1, 1)
                down_read(n, 0)
                if more:
                    p_split(n + 1, 2)
                down_add(n, 0, base)
                if more:
                    p_split(n + 1, 3)
                down_read(n, 1)
                down_add(n, 1, base)
                if s4:
                    s4_diagonal()
                    s4_maximum()
                    for i in range(TS):
                        conv_low(i)
                        if i == 1:
                            s4_split()
                if isinstance(n, int) and n == 0:
                    s4_vectors()
                    s4_inverse(0)
                for j in (2, 3):
                    down_read(n, j)
                    down_add(n, j, base)

            def low_rank_a():
                dve.wait_ge(s_lr, 16)
                V.tensor_scalar(a_w[:, :, 0:2 * R], a_raw, A_SCALE, None, ALU.mult).then_inc(s_ahi, 1)
                dve.wait_ge(s_ahi, 1)
                V.scalar_tensor_tensor(a_w[:, :, 2 * R:4 * R], a_raw, A_SCALE, a_w[:, :, 0:2 * R],
                                       ALU.mult, ALU.subtract).then_inc(s_aw, 1)

            def low_rank_b(g):
                w, last = (gb_w, ub_w)[g], slice(3 * R, 4 * R)
                dve.wait_ge(s_bhi[g], 1)
                V.scalar_tensor_tensor(w[last, :], b_raw[last, g, :], B_SCALE, w[last, :],
                                       ALU.mult, ALU.subtract).then_inc(s_bw, 1)

            def down_b():
                dve.wait_ge(s_lrd, 48)
                last = slice(3 * R, 4 * R)
                V.tensor_scalar(d_scale[:, :], d_scale[:, :], 0.5 * Q_STEP / H_SCALE, None, ALU.mult)
                V.tensor_scalar(db_w[:, :], db_raw, B_SCALE, None, ALU.mult).then_inc(s_dhi, 1)
                dve.wait_ge(s_dhi, 1)
                V.scalar_tensor_tensor(db_w[last, :], db_raw[last, :], B_SCALE, db_w[last, :],
                                       ALU.mult, ALU.subtract)

            def down_a():
                for slot in (0, 1, 3):
                    hi = V.tensor_scalar(da_w[:, :, slot, :], da_raw, A_SCALE, None, ALU.mult)
                hi.then_inc(s_dhi, 1)
                dve.wait_ge(s_dhi, 2)
                V.scalar_tensor_tensor(da_w[:, :, 2, :], da_raw, A_SCALE, da_w[:, :, 0, :],
                                       ALU.mult, ALU.subtract).then_inc(s_dw, 1)

            steps = [0]

            def link(ins):
                steps[0] += 1
                ins.then_inc(s_k, 1)
                dve.wait_ge(s_k, steps[0])

            def s4_vectors():
                dve.wait_ge(s_kin, 48)
                dve.wait_ge(s_bmm, 1)
                V.tensor_copy(rr[:, :, 0], bank[7][0:NS, 0:2])
                link(V.tensor_copy(rr[:, :, 1], pv))
                for i in range(2):
                    lr, li = lv[:, i, 0:1], lv[:, i, 1:2]
                    V.tensor_scalar(vt[:, 0, :], rr[:, 1, :], li, None, ALU.mult)
                    link(V.tensor_scalar(vt[:, 1, :], rr[:, 0, :], li, None, ALU.mult))
                    V.scalar_tensor_tensor(w1[:, 2 * i:2 * i + 2], rr[:, 0, :], lr, vt[:, 0, :],
                                           ALU.mult, ALU.add)
                    link(V.scalar_tensor_tensor(w1[:, 4 + 2 * i:6 + 2 * i], rr[:, 1, :], lr, vt[:, 1, :],
                                                ALU.mult, ALU.subtract))
                V.tensor_scalar(w2[:, 0:4], w1[:, 4:8], -1.0, None, ALU.mult)
                V.tensor_copy(w2[:, 4:8], w1[:, 0:4])

            def s4_inverse(half):
                dve.wait_ge(s_den, 1)
                cols = slice(half * L // 2, (half + 1) * L // 2)
                V.reciprocal(dsq[:, 1, cols], dsq[:, 0, cols]).then_inc(s_inverse, 1)

            def s4_resolvents():
                dve.wait_ge(s_inverse, 2)
                V.tensor_tensor(res[:, 0, :], den[:, 0, :], dsq[:, 1, :], ALU.mult)
                V.scalar_tensor_tensor(res[:, 1, :], den[:, 1, :], -1.0, dsq[:, 1, :],
                                       ALU.mult, ALU.mult).then_inc(s_res, 1)

            def product(o, ar, ai, br, bi):
                V.tensor_tensor(cw[:, 12, :], ar, br, ALU.mult)
                V.tensor_tensor(cw[:, 13, :], ai, bi, ALU.mult)
                V.tensor_tensor(cw[:, 14, :], ar, bi, ALU.mult)
                link(V.tensor_tensor(cw[:, 15, :], ai, br, ALU.mult))
                V.tensor_tensor(cw[:, o, :], cw[:, 12, :], cw[:, 13, :], ALU.subtract)
                link(V.tensor_tensor(cw[:, o + 1, :], cw[:, 14, :], cw[:, 15, :], ALU.add))

            def s4_sums():
                dve.wait_ge(s_cauchy, 1)
                link(V.tensor_copy(cs[:, :, :], bank[5][:, 0:8 * KH].rearrange("p (k c) -> p k c", c=8)))
                product(0, cs[:, :, 1], cs[:, :, 5], cs[:, :, 2], cs[:, :, 6])
                product(2, opk[:, 0, :], opk[:, 1, :], cw[:, 0, :], cw[:, 1, :])
                product(4, opk[:, 0, :], opk[:, 1, :], cs[:, :, 3], cs[:, :, 7])
                link(V.tensor_scalar(cw[:, 4, :], cw[:, 4, :], 1.0, None, ALU.add))

            def s4_roots():
                V.tensor_tensor(cw[:, 6, :], cw[:, 4, :], cw[:, 4, :], ALU.mult)
                link(V.tensor_tensor(cw[:, 7, :], cw[:, 5, :], cw[:, 5, :], ALU.mult))
                link(V.tensor_tensor(cw[:, 6, :], cw[:, 6, :], cw[:, 7, :], ALU.add))
                link(V.reciprocal(cw[:, 7, :], cw[:, 6, :]))
                V.tensor_tensor(cw[:, 8, :], cw[:, 4, :], cw[:, 7, :], ALU.mult)
                link(V.scalar_tensor_tensor(cw[:, 9, :], cw[:, 5, :], -1.0, cw[:, 7, :],
                                            ALU.mult, ALU.mult))
                product(10, cw[:, 2, :], cw[:, 3, :], cw[:, 8, :], cw[:, 9, :])
                V.tensor_tensor(cw[:, 0, :], cs[:, :, 0], cw[:, 10, :], ALU.subtract)
                link(V.tensor_tensor(cw[:, 1, :], cs[:, :, 4], cw[:, 11, :], ALU.subtract))
                link(V.tensor_scalar(cw[:, 2:4, :], cw[:, 0:2, :], 2.0 / (L * Z_SCALE), None, ALU.mult))

            def s4_phase(k0, k1):
                dve.wait_ge(s_tab, 32)
                for k in range(k0, k1):
                    at_r, at_i = cw[:, 2, k:k + 1], cw[:, 3, k:k + 1]
                    cos, sin = tab[:, 0, k, 0:P], tab[:, 1, k, 0:P]
                    V.tensor_scalar(ptmp[:, 0, :], sin, at_i, None, ALU.mult)
                    link(V.tensor_scalar(ptmp[:, 1, :], cos, at_i, None, ALU.mult))
                    V.scalar_tensor_tensor(phase[:, 0, k, :], cos, at_r, ptmp[:, 0, :], ALU.mult, ALU.add)
                    link(V.scalar_tensor_tensor(phase[:, 1, k, :], sin, at_r, ptmp[:, 1, :],
                                                ALU.mult, ALU.subtract))
                if k1 == KH:
                    V.tensor_scalar(d_col[:, :], step_in[:, 1:2], 1.0 / Z_SCALE, None, ALU.mult)\
                        .then_inc(s_phase, 1)

            def s4_diagonal():
                dve.wait_ge(s_phase, 1)
                dve.wait_ge(s_masked, 1)
                dve.wait_ge(s_ident, 2)
                V.scalar_tensor_tensor(toep[:, 0:P], ident[:, :], d_col[:, :], toep[:, 0:P],
                                       ALU.mult, ALU.add).then_inc(s_masked, 1)

            def s4_maximum():
                dve.wait_ge(s_masked, 2)
                V.tensor_reduce(k_max[:, :], toep[0:1, :], mybir.AxisListType.X, ALU.max,
                                apply_absolute_value=True).then_inc(s_max, 1)

            def s4_split():
                dve.wait_ge(s_maxmm, 1)
                link(V.tensor_scalar(k_scale[:, 0:1], bank[3][:, 0:1], 1e-30, 2.0 ** -13, ALU.max, ALU.mult))
                link(V.reciprocal(k_scale[:, 1:2], k_scale[:, 0:1]))
                link(V.tensor_scalar(toep[:, :], toep[:, :], k_scale[:, 1:2], None, ALU.mult))
                link(V.tensor_copy(toep16[:, 0, :], toep[:, :]))
                V.tensor_tensor(toep16[:, 1, :], toep[:, :], toep16[:, 0, :], ALU.subtract).then_inc(s_split, 1)

            def conv_low(i):
                b, j = i % 2, i % TS
                dve.wait_ge(c_zhi, i + 1)
                V.tensor_tensor(cz16[:, j, 1, :], czs[:, b, :], cz16[:, j, 0, :], ALU.subtract)\
                    .then_inc(c_z16, 1)

            def conv_add(i):
                j = i % TS
                dve.wait_ge(c_mm[j], i // TS + 1)
                V.scalar_tensor_tensor(X[:, i, :], c_bank[j][:, :], k_scale[:, 0:1], X[:, i, :],
                                       ALU.mult, ALU.add).then_inc(c_out[j], 1)

            for j in range(TS + 1):
                if j < TS:
                    dve.wait_ge(s_x[j], 16)
                    ln_stats(j, j, j)
                if j:
                    ln_apply(0, j - 1, j - 1)
            low_rank_a()
            p_split(0, 0)
            low_rank_b(0)
            p_split(0, 1)
            dve.wait_ge(s_scale_in, 16)
            V.tensor_scalar(scales[:, :, :], scales[:, :, :], Q_STEP / Z_SCALE, None, ALU.mult)\
                .then_inc(s_scales, 1)
            p_split(0, 2)
            p_split(0, 3)
            low_rank_b(1)
            tile(0, 0, True)
            dve.wait_ge(s_xrest[1], 16)
            with dve.Fori(1, TILES - 1) as n:
                tile(n, 0, True)
            tile(TILES - 1, 0, False, s4=True)

            for i in range(SUBS):
                if i in LN_STEP:
                    q = LN_STEP[i]
                    dve.wait_ge(c_out[q], 1)
                    ln_stats(SUBS + q, q, q)
                conv_add(i)
                if i - 1 in LN_STEP:
                    ln_apply(TILES, LN_STEP[i - 1], LN_STEP[i - 1])
                if i in P_STEP:
                    p_split(TILES, P_STEP[i])
            for j in range(TS):
                dve.wait_ge(c_out[j], SUBS // TS)
            tile(TILES, TILES, True)
            with dve.Fori(TILES + 1, 2 * TILES - 1) as n:
                tile(n, TILES, True)
            tile(2 * TILES - 1, TILES, False)

        @block.tensor
        def _(pe):
            mm = nc.tensor.matmul

            def x_transpose(j, k, bank_t):
                pe.wait_ge(f.z16, k + 1)
                after(pe, f.xT0, k - 1)
                dst = bank[bank_t][:, :].bitcast(F16).rearrange("p (a k t) -> p a k t", a=2, k=KH)
                for a in range(2):
                    for c in range(KH):
                        last = nc.tensor.transpose(dst[:, a, c, :], z16[:, j, a, c * P:(c + 1) * P],
                                                   ident16[:, :])
                last.then_inc(f.tp0, 1)

            def p_product(n, j):
                if isinstance(n, int) and n == 0:
                    pe.wait_ge(f.xT0, j + 1)
                else:
                    pe.wait_ge(f.xT[j], n * 16)
                if not (isinstance(n, int) and n == 0 and j < 3):
                    pe.wait_ge(f.p_stack, j - 2 if isinstance(n, int) and n == 0 else n * TS + j)
                for c in range(KH):
                    for a in range(2):
                        last = mm(p_bank(n, j)[:, 0:4 * R], xT[:, a, c, j * P:(j + 1) * P], a_w[:, c, :],
                                  start=(c == 0 and a == 0), stop=(c == KH - 1 and a == 1))
                last.then_inc(f.p_mm, 1)

            def p_transpose(j):
                pe.wait_ge(f.p_stack, j + 1)
                after(pe, f.PT0, j)
                for g in range(2):
                    last = nc.tensor.transpose(bank[7][:, g * P // 2:(g + 1) * P // 2].bitcast(F16),
                                               p_stack[:, j % 2, g, :, :].rearrange("p a r -> p (a r)"), ident16[:, :])
                last.then_inc(f.p_t0, 1)

            def pd_product(n, half):
                if half == 0:
                    pe.wait_ge(f.tg[(M - 1) % 2], uses(n, M - 1) + 1)
                    pe.wait_ge(f.hlo[0], uses(n, M - 3) + 1)
                    pe.wait_ge(f.hlo[1], uses(n, M - 4) + 1)
                for m in (range(0, DQ), range(DQ, M))[half]:
                    if m >= M - 2:
                        pe.wait_ge(f.hlo[m % 2], uses(n, m) + 1)
                    for a in range(2):
                        last = mm(bank[0][:, :], da_w[0:rows[m], m, :, :].rearrange("p a r -> p (a r)"),
                                  hT[0:rows[m], m, a, :], start=(m == 0 and a == 0),
                                  stop=(m == M - 1 and a == 1))
                if half:
                    last.then_inc(f.pd_mm, 1)

            def down_low(n, j):
                pe.wait_ge(f.pd_out, n + 1)
                after(pe, f.dsum, n * TS + j)
                mm(bank[6][:, :], PdT[:, j * P:(j + 1) * P], db_w[:, :], start=True, stop=True)\
                    .then_inc(f.dl_mm, 1)

            def down_half(n, j, half):
                b = j % 2
                if half == 0:
                    after(pe, f.d_read[b], n * 2 + j // 2)
                for m in (range(0, DQ), range(DQ, M))[half]:
                    if j == 0 and isinstance(n, int) and n == 0:
                        pe.wait_ge(s_dcast, m + 1)
                    for a in range(2):
                        last = mm(bank[4 + b][:, :], hT[0:rows[m], m, a, j * P:(j + 1) * P],
                                  dw[0:rows[m], m, :], start=(m == 0 and a == 0),
                                  stop=(m == M - 1 and a == 1))
                if half:
                    last.then_inc(f.d_mm[b], 1)

            def tile(n, more, s4=False, first=False):
                for m in range(M):
                    r, pb = rows[m], (m - 1) % 2 if m else (M - 1) % 2
                    before = uses(n, m - 1) + 1 if m else n * EVEN
                    cols = slice(m * P, m * P + r)
                    def product(g):
                        w, dst, done = ((gw, bank[0], f.g_mm), (uw, bank[1], f.u_mm))[g]
                        after(pe, (f.tg, f.tu)[g][pb], before)
                        if m == 0 and g == 1:
                            pe.wait_ge(f.p_stack, n * TS + TS)
                        if isinstance(n, int) and n == 0:
                            pe.wait_ge((s_gcast, s_ucast)[g], 1 + sum(m >= m1 for _, m1 in CHUNKS))
                        for c in range(KH):
                            for a in range(2):
                                last = mm(dst[0:r, :], w[:, c, cols], xT[:, a, c, :],
                                          start=(c == 0 and a == 0), stop=(c == KH - 1 and a == 1))
                        last.then_inc(done, 1)

                    def low_rank(g):
                        w, dst, done = ((gb_w, bank[2], f.gl_mm), (ub_w, bank[3], f.ul_mm))[g]
                        after(pe, (f.g, f.u)[g][pb], before)
                        if m == 0 and g == 0:
                            if isinstance(n, int) and n == 0:
                                pe.wait_ge(f.PT0, TS)
                            else:
                                for b in range(2):
                                    pe.wait_ge(f.PT[b], n * 32)
                        if isinstance(n, int) and n == 0 and m == 0:
                            pe.wait_ge(s_bw, g + 1)
                        if first and m == 0 and n != 0:
                            for out_read in c_out:
                                pe.wait_ge(out_read, SUBS // TS)
                        mm(dst[0:r, :], w[:, cols], PT[:, g, :], start=True, stop=True).then_inc(done, 1)

                    late = first and m == 0
                    started = late and n == 0
                    if not started:
                        product(0)
                    if not late:
                        low_rank(0)
                    if not started:
                        product(1)
                    if late:
                        low_rank(0)
                    low_rank(1)
                    if s4 and m == 2:
                        cauchy(n)
                if isinstance(n, int) and n == 0:
                    pe.wait_ge(s_dw, 1)
                    pe.wait_ge(s_kin, 48)
                    for c in range(2):
                        last = mm(bank[7][0:NS, c:c + 1], vct[:, c, :], bp, start=True, stop=True)
                    last.then_inc(s_bmm, 1)
                pd_product(n, 0)
                pd_product(n, 1)
                if more:
                    p_product(n + 1, 0)
                down_half(n, 0, 0)
                if more:
                    p_product(n + 1, 1)
                down_half(n, 0, 1)
                down_low(n, 0)
                down_half(n, 1, 0)
                if more:
                    p_product(n + 1, 2)
                if s4:
                    toeplitz(n)
                down_half(n, 1, 1)
                down_low(n, 1)
                if more:
                    p_product(n + 1, 3)
                for j in (2, 3):
                    down_half(n, j, 0)
                    down_half(n, j, 1)
                    down_low(n, j)
                    if s4 and j == 2:
                        toeplitz_max()

            def cauchy(n):
                pe.wait_ge(s_res, 1)
                pe.wait_ge(f.d_read[1], n * 2)
                for k in range(KH):
                    cols = slice(8 * k, 8 * k + 8)
                    mm(bank[5][:, cols], res[:, 0, k * P:(k + 1) * P], w1[:, :], start=True, stop=False)
                    last = mm(bank[5][:, cols], res[:, 1, k * P:(k + 1) * P], w2[:, :], start=False, stop=True)
                last.then_inc(s_cauchy, 1)

            def toeplitz(n):
                pe.wait_ge(s_phase, 1)
                for k in range(KH):
                    for c in range(2):
                        last = mm(bank[2][:, :], phase[:, c, k, :], tab[:, c, k, :],
                                  start=(k == 0 and c == 0), stop=(k == KH - 1 and c == 1))
                last.then_inc(s_toep, 1)

            def toeplitz_max():
                pe.wait_ge(s_const, 4)
                pe.wait_ge(s_max, 1)
                mm(bank[3][:, 0:1], ones[:, :], k_max[:, :], start=True, stop=True).then_inc(s_maxmm, 1)

            def conv_product(i):
                j = i % TS
                pe.wait_ge(c_zT[i % (2 * TS)], i // (2 * TS) * 16 + 16)
                if i < 2:
                    pe.wait_ge(f.d_read[i], 2 * TILES)
                after(pe, c_out[j], i // TS)
                for c in range(KH):
                    for a, t in (0, 0), (1, 0), (0, 1):
                        last = mm(c_bank[j][:, c * P:L], czT[i // TS % 2][:, j, a, c, :],
                                  toep16[:, t, 0:L - c * P],
                                  start=(c == 0 and a == 0 and t == 0), stop=(c == KH - 1 and t == 1))
                last.then_inc(c_mm[j], 1)

            pe.wait_ge(s_ident, 2)
            def first_products(j):
                pe.wait_ge(f.xT0, j + 1)
                cols = slice(j * P, (j + 1) * P)
                for g, w in enumerate((gw, uw)):
                    pe.wait_ge((s_gcast, s_ucast)[g], 1)
                    for c in range(KH):
                        for a in range(2):
                            last = mm(bank[g][:, cols], w[:, c, 0:P], xT[:, a, c, cols],
                                      start=(c == 0 and a == 0), stop=(c == KH - 1 and a == 1))
                    if j == TS - 1:
                        last.then_inc((f.g_mm, f.u_mm)[g], 1)

            x_transpose(0, 0, 2)
            x_transpose(1, 1, 3)
            first_products(0)
            x_transpose(2, 2, 2)
            first_products(1)
            x_transpose(3, 3, 3)
            pe.wait_ge(s_aw, 1)
            p_product(0, 0)
            p_product(0, 1)
            p_transpose(0)
            first_products(2)
            p_product(0, 2)
            p_transpose(1)
            p_product(0, 3)
            first_products(3)
            p_transpose(2)
            p_transpose(3)
            tile(0, True, first=True)
            with pe.Fori(1, TILES - 1) as n:
                tile(n, True)
            tile(TILES - 1, False, s4=True)

            pe.wait_ge(s_split, 1)
            for i in range(SUBS):
                conv_product(i)
                if i in P_STEP:
                    p_product(TILES, P_STEP[i])
            tile(TILES, True, first=True)
            with pe.Fori(TILES + 1, 2 * TILES - 1) as n:
                tile(n, True)
            tile(2 * TILES - 1, False)


_OUT = ((2, 1024, 512), "float32")


def kernel(**inputs):
    import numpy as _np
    import concourse.bacc as _bacc
    from concourse import mybir as _mybir
    from concourse.bass_utils import run_bass_kernel_spmd as _run

    a = {k: _np.asarray(v) for k, v in inputs.items()}
    H = a["L0_attn_u"].shape[-1]
    I = a["L0_ffn_gate_q"].shape[0]
    M = -(-I // P)

    def columns(v):
        padded = _np.zeros(M * P, v.dtype)
        padded[:I] = v
        return padded.reshape(M, P).T

    down_a = _np.zeros((M * P, a["L0_ffn_down_A"].shape[1]), a["L0_ffn_down_A"].dtype)
    down_a[:I] = a["L0_ffn_down_A"]
    down_a = down_a.reshape(M, P, -1).transpose(1, 0, 2)
    vc = a["L0_attn_Vc_ri"].transpose(1, 2, 0)
    state = _np.concatenate([a["L0_attn_Lambda_ri"], a["L0_attn_p_ri"], a["L0_attn_Ct_ri"][0],
                             a["L0_attn_q_ri"], a["L0_attn_Bp"], vc.reshape(len(vc), -1)], axis=1)

    k = _np.arange(H, dtype=_np.float64)
    w = _np.exp(-2j * _np.pi * k / H)
    omega = _np.stack([1 - w.real, 1 + w.real, w.imag]).astype(_np.float32)
    opk = _np.stack([1 + w.real, w.imag]).reshape(2, H // P, P).transpose(2, 0, 1).astype(_np.float32)
    angle = 2 * _np.pi * (_np.outer(_np.arange(H), _np.arange(H)) % H) / H
    tab = _np.stack([_np.cos(angle), _np.sin(angle)]).astype(_np.float32)

    data = [
        ("x", a["L0_attn_u"].reshape(-1, H)), ("state", state),
        ("log_step_d", _np.concatenate([a["L0_attn_log_step"], a["L0_attn_D"]])),
        ("gate_q_t", a["L0_ffn_gate_q"].T), ("up_q_t", a["L0_ffn_up_q"].T),
        ("down_q_t", a["L0_ffn_down_q"].T),
        ("scales", _np.stack([columns(a["L0_ffn_gate_scale"]), columns(a["L0_ffn_up_scale"])], axis=1)),
        ("down_scale", a["L0_ffn_down_scale"]),
        ("a", _np.concatenate([a["L0_ffn_gate_A"], a["L0_ffn_up_A"]], axis=1)),
        ("b", _np.tile(_np.stack([a["L0_ffn_gate_B"], a["L0_ffn_up_B"]], axis=1), (4, 1, 1))),
        ("down_a", down_a), ("down_b", _np.tile(a["L0_ffn_down_B"], (4, 1))),
        ("omega", omega), ("one_plus_omega", opk), ("tables", tab),
    ]
    nc = _bacc.Bacc("TRN2", target_bir_lowering=False, num_devices=1)
    arrays, args = {}, []
    for name, v in data:
        v = _np.ascontiguousarray(v)
        arrays[f"in_{name}"] = v
        args.append(nc.dram_tensor(f"in_{name}", v.shape, _mybir.dt.from_np(v.dtype), kind="ExternalInput").ap())
    shape, dtype = _OUT
    out = nc.dram_tensor("out_x", (shape[0] * shape[1], shape[2]), _mybir.dt.from_np(_np.dtype(dtype)),
                         kind="ExternalOutput").ap()
    s4_macaron(nc, *args, out)
    r = _run(nc, [arrays], core_ids=[0])
    return r.results[0]["out_x"].reshape(shape)
```
